# Optimizing a Trainium2 kernel written in Bass

```python
import numpy as np
import jax
import jax.numpy as jnp

def _softmax(x, axis=-1):
    return jax.nn.softmax(x, axis=axis)

def _gelu(x):
    return jax.nn.gelu(x, approximate=True)

def _silu(x):
    return jax.nn.silu(x)

def _sigmoid(x):
    return jax.nn.sigmoid(x)

def _layernorm(x, axis=-1, eps=1e-05):
    m = jnp.mean(x, axis=axis, keepdims=True)
    v = jnp.var(x, axis=axis, keepdims=True)
    return (x - m) / jnp.sqrt(v + eps)

def _scatter_add(tgt, idx, src, axis=0):
    return tgt.at[idx].add(src)

def _segment_sum(src, seg, n):
    return jax.ops.segment_sum(src, seg, n)
kernel_name = 'mk_adj_resnorm_d4_adj_r2_f2e012'

def setup_inputs(seed: int=0):
    np.random.seed(seed)
    _w = jnp.asarray

    def _rec_inputs():
        import jax
        import jax.numpy as jnp
        _gk = jax.random.key(seed)
        x = -0.0003929 + 0.9999 * jax.random.normal(jax.random.fold_in(_gk, 1), (32, 256, 256), jnp.float32)
        _w = (1.0 + jnp.arange(256, dtype=jnp.float32)) ** (-0.5)
        _w = _w / _w.mean()
        _pij = jnp.clip(0.0078125 * _w[:, None] * _w[None, :], 0.0, 1.0)
        _a = jax.random.uniform(jax.random.fold_in(_gk, 2), (256, 256)) < _pij
        _a = jnp.logical_or(_a, jnp.eye(256, dtype=bool))
        _af = _a.astype(jnp.float32)
        _af = _af * jax.random.uniform(jax.random.fold_in(_gk, 3), (256, 256), jnp.float32, 0.05, 1)
        adj = _af
        return (x, adj)
    x, adj = _rec_inputs()

    def _L0_gnn_setup():
        import jax, jax.numpy as jnp
        import numpy as np
        B, N, D, O = (8, 2048, 256, 256)
        key = jax.random.key(seed)
        k1, k2, k3, k4 = jax.random.split(key, 4)
        x = jax.random.normal(k1, (B, N, D), dtype=jnp.float32)
        adj = jax.random.uniform(k2, (N, N), dtype=jnp.float32)
        weight = jax.random.normal(k3, (D, O), dtype=jnp.float32) * 0.02
        bias = jax.random.normal(k4, (O,), dtype=jnp.float32) * 0.02
        return {'x': x, 'adj': adj, 'weight': weight, 'bias': bias}
    _L0_gnn_all = _L0_gnn_setup()
    _L0_gnn_in = {k: v for k, v in _L0_gnn_all.items() if k in ('weight', 'bias')}
    del _L0_gnn_all

    def _L1_gnn_setup():
        import jax, jax.numpy as jnp
        import numpy as np
        B, N, D, T = (64, 128, 256, 3)

        def _lin(v, W, b):
            return jnp.einsum('...i,oi->...o', v, W) + b
        key = jax.random.key(seed)
        ks = jax.random.split(key, 12)
        s2 = 1.0 / np.sqrt(2 * D)
        s1 = 1.0 / np.sqrt(D)
        return {'x': jax.random.normal(ks[0], (B, N, D), jnp.float32), 'in_mat': jax.random.uniform(ks[1], (N, N), jnp.float32) / N, 'out_mat': jax.random.uniform(ks[2], (N, N), jnp.float32) / N, 'w3_w': jax.random.normal(ks[3], (D, 2 * D), jnp.float32) * s2, 'w3_b': jnp.zeros((D,), jnp.float32), 'u3_w': jax.random.normal(ks[4], (D, D), jnp.float32) * s1, 'u3_b': jnp.zeros((D,), jnp.float32), 'w4_w': jax.random.normal(ks[5], (D, 2 * D), jnp.float32) * s2, 'w4_b': jnp.zeros((D,), jnp.float32), 'w5_w': jax.random.normal(ks[6], (D, 2 * D), jnp.float32) * s2, 'w5_b': jnp.zeros((D,), jnp.float32), 'u5_w': jax.random.normal(ks[7], (D, D), jnp.float32) * s1, 'u5_b': jnp.zeros((D,), jnp.float32)}
    _L1_gnn_all = _L1_gnn_setup()
    _L1_gnn_in = {k: v for k, v in _L1_gnn_all.items() if k in ('w3_w', 'w3_b', 'u3_w', 'u3_b', 'w4_w', 'w4_b', 'w5_w', 'w5_b', 'u5_w', 'u5_b')}
    del _L1_gnn_all

    def _L2_gnn_setup():
        import jax, jax.numpy as jnp
        import numpy as np
        B, N, D, H = (4, 1024, 256, 8)
        HD = D // H
        key = jax.random.key(seed)
        ks = jax.random.split(key, 10)
        x = jax.random.normal(ks[0], (B, N, D), dtype=jnp.float32)
        adj = (jax.random.uniform(ks[1], (N, N)) < 0.1).astype(jnp.float32)
        s = 1.0 / np.sqrt(D)
        Wq = jax.random.normal(ks[2], (D, D), dtype=jnp.float32) * s
        Wk = jax.random.normal(ks[3], (D, D), dtype=jnp.float32) * s
        Wv = jax.random.normal(ks[4], (D, D), dtype=jnp.float32) * s
        Wo = jax.random.normal(ks[5], (D, D), dtype=jnp.float32) * s
        bq = jnp.zeros((D,), jnp.float32)
        bk = jnp.zeros((D,), jnp.float32)
        bv = jnp.zeros((D,), jnp.float32)
        bo = jnp.zeros((D,), jnp.float32)
        return {'x': x, 'adj': adj, 'Wq': Wq, 'bq': bq, 'Wk': Wk, 'bk': bk, 'Wv': Wv, 'bv': bv, 'Wo': Wo, 'bo': bo}
    _L2_gnn_all = _L2_gnn_setup()
    _L2_gnn_in = {k: v for k, v in _L2_gnn_all.items() if k in ('Wq', 'bq', 'Wk', 'bk', 'Wv', 'bv', 'Wo', 'bo')}
    del _L2_gnn_all

    def _L3_gnn_setup():
        import jax, jax.numpy as jnp
        import numpy as np
        B, N, D, H = (16, 1025, 256, 8)
        LN_EPS = 1e-05

        def _make_mask(key, n):
            n_proto = n - 1
            adj = jax.random.bernoulli(key, 0.03, (n_proto, n_proto)).astype(jnp.float32)
            adj = jnp.clip(adj + adj.T + jnp.eye(n_proto, dtype=jnp.float32), 0.0, 1.0)
            mask = jnp.zeros((n, n), dtype=jnp.float32)
            mask = mask.at[0, :].set(1.0).at[:, 0].set(1.0)
            mask = mask.at[1:, 1:].set(adj)
            return mask
        key = jax.random.key(seed)
        ks = jax.random.split(key, 7)
        s = 1.0 / np.sqrt(D)
        return {'x': jax.random.normal(ks[0], (B, N, D), dtype=jnp.float32), 'w_qkv': jax.random.uniform(ks[1], (D, 3 * D), dtype=jnp.float32, minval=-s, maxval=s), 'w_proj': jax.random.uniform(ks[2], (D, D), dtype=jnp.float32, minval=-s, maxval=s), 'b_proj': jnp.zeros((D,), dtype=jnp.float32), 'ln_gamma': jnp.ones((D,), dtype=jnp.float32), 'ln_beta': jnp.zeros((D,), dtype=jnp.float32), 'attn_mask': _make_mask(ks[3], N)}
    _L3_gnn_all = _L3_gnn_setup()
    _L3_gnn_in = {k: v for k, v in _L3_gnn_all.items() if k in ('w_qkv', 'w_proj', 'b_proj', 'ln_gamma', 'ln_beta')}
    del _L3_gnn_all
    return {'x': x, 'adj': adj, 'L0_gnn_weight': _L0_gnn_in['weight'], 'L0_gnn_bias': _L0_gnn_in['bias'], 'L1_gnn_w3_w': _L1_gnn_in['w3_w'], 'L1_gnn_w3_b': _L1_gnn_in['w3_b'], 'L1_gnn_u3_w': _L1_gnn_in['u3_w'], 'L1_gnn_u3_b': _L1_gnn_in['u3_b'], 'L1_gnn_w4_w': _L1_gnn_in['w4_w'], 'L1_gnn_w4_b': _L1_gnn_in['w4_b'], 'L1_gnn_w5_w': _L1_gnn_in['w5_w'], 'L1_gnn_w5_b': _L1_gnn_in['w5_b'], 'L1_gnn_u5_w': _L1_gnn_in['u5_w'], 'L1_gnn_u5_b': _L1_gnn_in['u5_b'], 'L2_gnn_Wq': _L2_gnn_in['Wq'], 'L2_gnn_bq': _L2_gnn_in['bq'], 'L2_gnn_Wk': _L2_gnn_in['Wk'], 'L2_gnn_bk': _L2_gnn_in['bk'], 'L2_gnn_Wv': _L2_gnn_in['Wv'], 'L2_gnn_bv': _L2_gnn_in['bv'], 'L2_gnn_Wo': _L2_gnn_in['Wo'], 'L2_gnn_bo': _L2_gnn_in['bo'], 'L3_gnn_w_qkv': _L3_gnn_in['w_qkv'], 'L3_gnn_w_proj': _L3_gnn_in['w_proj'], 'L3_gnn_b_proj': _L3_gnn_in['b_proj'], 'L3_gnn_ln_gamma': _L3_gnn_in['ln_gamma'], 'L3_gnn_ln_beta': _L3_gnn_in['ln_beta']}

def reference(x, adj, L0_gnn_weight, L0_gnn_bias, L1_gnn_w3_w, L1_gnn_w3_b, L1_gnn_u3_w, L1_gnn_u3_b, L1_gnn_w4_w, L1_gnn_w4_b, L1_gnn_w5_w, L1_gnn_w5_b, L1_gnn_u5_w, L1_gnn_u5_b, L2_gnn_Wq, L2_gnn_bq, L2_gnn_Wk, L2_gnn_bk, L2_gnn_Wv, L2_gnn_bv, L2_gnn_Wo, L2_gnn_bo, L3_gnn_w_qkv, L3_gnn_w_proj, L3_gnn_b_proj, L3_gnn_ln_gamma, L3_gnn_ln_beta):
    import jax
    import jax.numpy as jnp

    def _L0_gnn_ref(x, adj, weight, bias):
        import jax, jax.numpy as jnp
        import numpy as np
        B, N, D, O = (8, 2048, 256, 256)
        y = jnp.einsum('nm,bmd->bnd', adj, x)
        out = jnp.einsum('bnd,do->bno', y, weight) + bias
        return out

    def _L1_gnn_ref(x, in_mat, out_mat, w3_w, w3_b, u3_w, u3_b, w4_w, w4_b, w5_w, w5_b, u5_w, u5_b):
        import jax, jax.numpy as jnp
        import numpy as np
        B, N, D, T = (64, 128, 256, 3)

        def _lin(v, W, b):
            return jnp.einsum('...i,oi->...o', v, W) + b
        h = x
        for _ in range(T):
            a_in = jnp.einsum('nm,bmd->bnd', in_mat, h)
            a_out = jnp.einsum('nm,bmd->bnd', out_mat, h)
            av = jnp.concatenate([a_in, a_out], axis=-1)
            z = jax.nn.sigmoid(_lin(av, w3_w, w3_b) + _lin(h, u3_w, u3_b))
            r = jax.nn.sigmoid(_lin(av, w4_w, w4_b) + _lin(h, u3_w, u3_b))
            hv = jnp.tanh(_lin(av, w5_w, w5_b) + _lin(r * h, u5_w, u5_b))
            h = (1.0 - z) * h + z * hv
        return h

    def _L2_gnn_ref(x, adj, Wq, bq, Wk, bk, Wv, bv, Wo, bo):
        import jax, jax.numpy as jnp
        import numpy as np
        B, N, D, H = (4, 1024, 256, 8)
        HD = D // H
        b, n, d = x.shape
        q = (x @ Wq + bq).reshape(b, n, H, HD)
        k = (x @ Wk + bk).reshape(b, n, H, HD)
        v = (x @ Wv + bv).reshape(b, n, H, HD)
        scores = jnp.einsum('bqhd,bkhd->bhqk', q, k) / jnp.sqrt(jnp.float32(HD))
        scores = scores + (1.0 - adj)[None, None, :, :] * -1000000000.0
        attn = jax.nn.softmax(scores, axis=-1)
        out = jnp.einsum('bhqk,bkhd->bqhd', attn, v).reshape(b, n, d)
        return out @ Wo + bo

    def _L3_gnn_ref(x, w_qkv, w_proj, b_proj, ln_gamma, ln_beta, attn_mask):
        import jax, jax.numpy as jnp
        import numpy as np
        B, N, D, H = (16, 1025, 256, 8)
        LN_EPS = 1e-05

        def _make_mask(key, n):
            n_proto = n - 1
            adj = jax.random.bernoulli(key, 0.03, (n_proto, n_proto)).astype(jnp.float32)
            adj = jnp.clip(adj + adj.T + jnp.eye(n_proto, dtype=jnp.float32), 0.0, 1.0)
            mask = jnp.zeros((n, n), dtype=jnp.float32)
            mask = mask.at[0, :].set(1.0).at[:, 0].set(1.0)
            mask = mask.at[1:, 1:].set(adj)
            return mask
        b, n, d = x.shape
        hd = d // H
        scale = hd ** (-0.5)
        qkv = (x @ w_qkv).reshape(b, n, 3, H, hd).transpose(2, 0, 3, 1, 4)
        q, k, v = (qkv[0], qkv[1], qkv[2])
        attn = jnp.einsum('bhnd,bhmd->bhnm', q, k) * scale
        attn = jnp.where(attn_mask[None, None] == 0, -jnp.inf, attn)
        attn = jax.nn.softmax(attn, axis=-1)
        o = jnp.einsum('bhnm,bhmd->bhnd', attn, v).transpose(0, 2, 1, 3).reshape(b, n, d)
        o = o @ w_proj + b_proj
        mu = jnp.mean(o, axis=-1, keepdims=True)
        var = jnp.mean(jnp.square(o - mu), axis=-1, keepdims=True)
        ln = (o - mu) * jax.lax.rsqrt(var + LN_EPS) * ln_gamma + ln_beta
        return o + ln
    x = _layernorm(x + _L0_gnn_ref(x, adj, L0_gnn_weight, L0_gnn_bias), axis=-1)
    x = _layernorm(x + _L1_gnn_ref(x, adj, adj, L1_gnn_w3_w, L1_gnn_w3_b, L1_gnn_u3_w, L1_gnn_u3_b, L1_gnn_w4_w, L1_gnn_w4_b, L1_gnn_w5_w, L1_gnn_w5_b, L1_gnn_u5_w, L1_gnn_u5_b), axis=-1)
    x = _layernorm(x + _L2_gnn_ref(x, adj, L2_gnn_Wq, L2_gnn_bq, L2_gnn_Wk, L2_gnn_bk, L2_gnn_Wv, L2_gnn_bv, L2_gnn_Wo, L2_gnn_bo), axis=-1)
    x = _layernorm(x + _L3_gnn_ref(x, L3_gnn_w_qkv, L3_gnn_w_proj, L3_gnn_b_proj, L3_gnn_ln_gamma, L3_gnn_ln_beta, adj), axis=-1)
    return x

_drawn_inputs = setup_inputs


def setup_inputs(seed=0):
    import zlib

    import numpy as np

    out = dict(_drawn_inputs(seed))
    spreads = {'L1_gnn_w3_b': (0.0, 0.357),
     'L1_gnn_u3_b': (0.0, 0.328),
     'L1_gnn_w4_b': (0.0, 0.8),
     'L1_gnn_w5_b': (0.0, 0.1),
     'L1_gnn_u5_b': (0.0, 0.1),
     'L2_gnn_bq': (0.0, 0.1),
     'L2_gnn_bk': (0.0, 0.1),
     'L2_gnn_bv': (0.0, 0.1),
     'L2_gnn_bo': (0.0, 0.1),
     'L3_gnn_b_proj': (0.0, 0.1),
     'L3_gnn_ln_gamma': (1.0, 0.2),
     'L3_gnn_ln_beta': (0.0, 0.1)}
    factors = {}
    for name, (base, spread) in spreads.items():
        noise = np.random.default_rng([zlib.crc32(name.encode()), seed]).standard_normal(out[name].shape)
        drawn = base * np.exp(spread * noise) if base else spread * noise
        out[name] = jnp.asarray(drawn.astype(out[name].dtype))
    for name, factor in factors.items():
        out[name] = (out[name] * factor).astype(out[name].dtype)
    return out
```

```python
import concourse.bass as bass
from concourse import mybir
from contextlib import ExitStack
import math

B, N, D, H = 32, 256, 256, 8
HD = D // H
P = 128
GRAPHS = 2
COLS = GRAPHS * N
GROUPS = B // GRAPHS
RT = COLS // P
KT = D // P
STEPS = 3
UNITS = RT * H // 2
EPS = 1e-5
WS = 64.0
QK = 1.0 / math.sqrt(HD)
MASK_L2 = 1e9
MASK_L3 = 3.0e38

PER = dict(
    x_loaded=16, xb=1, hn_hi=8, hn_lo=8, fill_x=22, fill_y=14, af_hi=8, af_lo=8, res_a=4,
    hf32=2, hf_hi=6, hf_lo=6, tr=6, tz=6, tv=6, rh=6, rh_hi=6, rh_lo=6, dif=6, upd=6, hf_new=6,
    a_st=8, a_mv=8, a_ve=2, a_rs=2, a_ln=8,
    xb2=1, xf_fill=4, xf_hi=4, xf_lo=4, qk_fill=8, q_hi=4, q_lo=4, k_hi=4, k_lo=4,
    v_fill=4, v_hi=4, v_lo=4, stack=2 * 24 * 16, s_fill=2 * UNITS, s_min=4 * UNITS, p_exp=4 * UNITS, pt_fill=2 * UNITS,
    pt_hi=2 * UNITS, pt_lo=2 * UNITS, pv=2 * UNITS, rec=8, norm=8, of_fill=4, of_hi=4, of_lo=4, o_fill=4, res_b=4,
    gam=1, xbe=1, obe=1, t_fin=1,
    b_st=12, b_mv=12, b_ve=3, b_rs=3, b_ln=12, stored=16,
)

MATS = ["adjT", "w0", "w3", "w4", "w5", "u3", "u5", "q2", "k2", "v2", "o2", "q3", "k3", "v3", "o3"]
SCALE = {m: WS for m in MATS}
SCALE.update(adjT=1.0, u5=WS / 2, q2=-WS * QK, q3=-WS * QK)


def gnn_stack_kernel(nc, x, adj, adjT, w0, b0, w3T, b3, u3T, bu3, w4T, b4, w5T, b5, u5T, bu5,
                     wq, bq, wk, bk, wv, bv, wo, bo, wqkv, wproj, bproj, gamma, beta, out):
    f32, f16 = mybir.dt.float32, mybir.dt.float16
    ALU = mybir.AluOpType
    ACT = mybir.ActivationFunctionType

    x_v = x.rearrange("(g t p) d -> g p t d", t=RT, p=P)
    out_v = out.rearrange("(g t p) d -> g p t d", t=RT, p=P)

    def rows(m):
        return m.rearrange("(t p) n -> p t n", p=P)

    ctx = ExitStack()
    with ctx:
        def sb(name, shape, dt=f32):
            return ctx.enter_context(nc.sbuf_tensor(name, shape, dt))

        def sem(name):
            return ctx.enter_context(nc.semaphore(name))

        W_hi = sb("W_hi", [P, len(MATS), KT, D], f16)
        W_lo = sb("W_lo", [P, len(MATS), KT, D], f16)
        bufs = sb("bufs", [P, 10, RT, D])
        x3, tB, o_n, o_g, xbe, obe, tF, y_out, xb2, oN = (bufs[:, i] for i in range(10))
        raw = bufs[:, 0:8].rearrange("p s (m k) d -> p (s m) k d", k=KT)
        raw2 = bufs[:, 8:10].rearrange("p s (m k) d -> p (s m) k d", k=KT)
        adj_sb = sb("adj_sb", [P, KT, N])
        neg_mask = sb("neg_mask", [P, 2, KT, N])
        rep = sb("rep", [P, 5, D])
        b0_r, bo_r, bp_r, gam_r, bet_r = (rep[:, i, :] for i in range(5))
        bias_in = sb("bias_in", [P, 8, KT])
        bias = sb("bias", [P, 5, KT])
        ident = sb("ident", [P, P])
        m_half = sb("m_half", [P, RT])
        eps_t = sb("eps_t", [P, RT])
        xin = sb("xin", [P, RT, D])
        xb = sb("xb", [P, RT, D])
        hn_hi = sb("hn_hi", [P, RT, D], f16)
        hn_lo = sb("hn_lo", [P, RT, D], f16)
        af_hi = sb("af_hi", [P, KT, COLS], f16)
        af_lo = sb("af_lo", [P, KT, COLS], f16)
        hF = sb("hF", [P, KT, COLS])
        hf_hi = sb("hf_hi", [P, KT, COLS], f16)
        hf_lo = sb("hf_lo", [P, KT, COLS], f16)
        trb = sb("trb", [P, KT, COLS])
        tzb = sb("tzb", [P, KT, COLS])
        tvb = sb("tvb", [P, KT, COLS])
        rhb = sb("rhb", [P, KT, COLS])
        rh_hi = sb("rh_hi", [P, KT, COLS], f16)
        rh_lo = sb("rh_lo", [P, KT, COLS], f16)
        difb = sb("difb", [P, KT, COLS])
        updb = sb("updb", [P, KT, COLS])
        tA = sb("tA", [P, RT, D])
        x1 = sb("x1", [P, RT, D])
        stA = sb("stA", [P, RT, 6])
        mvA = sb("mvA", [P, RT, 2])
        veA = sb("veA", [P, RT])
        rsA = sb("rsA", [P, RT])
        x2 = sb("x2", [P, RT, D])
        xf_hi = sb("xf_hi", [P, KT, COLS], f16)
        xf_lo = sb("xf_lo", [P, KT, COLS], f16)
        q_hi = sb("q_hi", [P, KT, COLS], f16)
        q_lo = sb("q_lo", [P, KT, COLS], f16)
        k_hi = sb("k_hi", [P, KT, COLS], f16)
        k_lo = sb("k_lo", [P, KT, COLS], f16)
        qs = sb("qs", [3 * HD, H, COLS], f16)
        ks = sb("ks", [3 * HD, H, COLS], f16)
        v_hi = sb("v_hi", [P, RT, H, HD + 2], f16)
        v_lo = sb("v_lo", [P, RT, H, HD], f16)
        sp = sb("sp", [P, 3, 2, N])
        s_min = sb("s_min", [P, 3, 2])
        p_sb = sb("p_sb", [P, 2, 2, N])
        pt_hi = sb("pt_hi", [P, 2, 2 * KT * P], f16)
        pt_lo = sb("pt_lo", [P, 2, 2 * KT * P], f16)
        rec = sb("rec", [P, 2, H])
        of_hi = sb("of_hi", [P, KT, COLS], f16)
        of_lo = sb("of_lo", [P, KT, COLS], f16)
        stB = sb("stB", [P, RT, 6])
        mvB = sb("mvB", [P, RT, 2])
        veB = sb("veB", [P, RT])
        rsB = sb("rsB", [P, RT])

        psum = [ctx.enter_context(nc.psum_tensor(f"bank{i}", [P, COLS], f32)) for i in range(8)]
        X, Y = psum[0:2], psum[2:4]
        SB, PTB, OB = psum[4:6], psum[6], psum[7]

        S = {name: sem(name) for name in PER}
        w_in, w_set, w_hi_s, w_lo_s, id_s, one_s, half_s, masks_ready = (
            sem(n) for n in ("w_in", "w_set", "w_hi_done", "w_lo_done", "ident_ready", "ones_ready", "half_ready", "masks_ready"))
        passed = sem("passed")

        def has_before(g):
            return not isinstance(g, int) or g > 0

        def at(name, g, k):
            return g * PER[name] + k

        def settled(eng):
            eng.sem_inc(passed, 1)

        MI = {m: i for i, m in enumerate(MATS)}

        def w(m):
            i = MI[m]
            return W_hi[:, i], W_lo[:, i]

        def mm3(o, l, r, start, stop):
            (lh, ll), (rh_, rl) = l, r
            nc.tensor.matmul(o, lh, rh_, start=start, stop=False)
            nc.tensor.matmul(o, lh, rl, start=False, stop=False)
            return nc.tensor.matmul(o, ll, rh_, start=False, stop=stop)

        def by_feature(bank, m, act, t, start, stop):
            wh, wl = w(m)
            c = slice(t * P, t * P + P)
            for k in range(KT):
                last = mm3(bank[t][:, :], (wh[:, k, c], wl[:, k, c]),
                           (act[0][:, k, :], act[1][:, k, :]),
                           start and k == 0, stop and k == KT - 1)
            return last

        def by_node(bank, m, act, j):
            wh, wl = w(m)
            for i in range(2):
                c = slice((2 * j + i) * P, (2 * j + i + 1) * P)
                for k in range(KT):
                    last = mm3(bank[j][:, i * D:(i + 1) * D], (act[0][:, k, c], act[1][:, k, c]),
                               (wh[:, k, :], wl[:, k, :]), k == 0, k == KT - 1)
            return last

        def adj_product(t):
            ah, al = w("adjT")
            for b in range(GRAPHS):
                for k in range(KT):
                    r = b * KT + k
                    last = mm3(X[t][:, b * N:(b + 1) * N],
                               (hn_hi[:, r, t * P:(t + 1) * P], hn_lo[:, r, t * P:(t + 1) * P]),
                               (ah[:, k, :], al[:, k, :]), k == 0, k == KT - 1)
            return last

        def to_features(bank, src, t):
            for r in range(RT):
                last = nc.tensor.transpose(bank[t][:, r * P:(r + 1) * P], src[:, r, t * P:(t + 1) * P], ident[:, :])
            return last

        def to_nodes(bank, src, j):
            for i in range(2):
                r = 2 * j + i
                for t in range(KT):
                    last = nc.tensor.transpose(bank[j][:, i * D + t * P:i * D + (t + 1) * P],
                                               src[:, t, r * P:(r + 1) * P], ident[:, :])
            return last

        AF, HF, RH = (af_hi, af_lo), (hf_hi, hf_lo), (rh_hi, rh_lo)

        def pe_a(pe, g):
            later = has_before(g)
            for t in range(KT):
                if t == 0:
                    pe.wait_ge(S["hn_hi"], at("hn_hi", g, 2))
                    pe.wait_ge(S["hn_lo"], at("hn_lo", g, 2))
                    if later:
                        pe.wait_ge(S["res_a"], at("res_a", g, 0))
                adj_product(t).then_inc(S["fill_x"], 1)
                yield
            pe.wait_ge(S["af_hi"], at("af_hi", g, 2))
            pe.wait_ge(S["af_lo"], at("af_lo", g, 2))
            if later:
                pe.wait_ge(S["tv"], at("tv", g, 0))
            for j in range(2):
                by_node(Y, "w0", AF, j).then_inc(S["fill_y"], 1)
                yield
            pe.wait_ge(S["a_ln"], at("a_ln", g, 4))
            for t in range(KT):
                to_features(X, x1, t).then_inc(S["fill_x"], 1)
            yield
            for s in range(STEPS):
                pe.wait_ge(S["hn_hi"], at("hn_hi", g, 4 + 2 * s))
                pe.wait_ge(S["hn_lo"], at("hn_lo", g, 4 + 2 * s))
                pe.wait_ge(S["hf_hi"], at("hf_hi", g, 2 + 2 * s))
                pe.wait_ge(S["hf_lo"], at("hf_lo", g, 2 + 2 * s))
                pe.wait_ge(S["hf32"], at("hf32", g, 2))
                for t in range(KT):
                    adj_product(t).then_inc(S["fill_x"], 1)
                    yield
                if s == 0:
                    pe.wait_ge(S["res_a"], at("res_a", g, 2))
                else:
                    if later or 2 * s > 0:
                        pe.wait_ge(S["tv"], at("tv", g, 2 * s))
                for t in range(KT):
                    by_feature(Y, "u3", HF, t, True, False)
                    yield
                pe.wait_ge(S["af_hi"], at("af_hi", g, 4 + 2 * s))
                pe.wait_ge(S["af_lo"], at("af_lo", g, 4 + 2 * s))
                for t in range(KT):
                    by_feature(Y, "w4", AF, t, False, True).then_inc(S["fill_y"], 1)
                    yield
                for t in range(KT):
                    by_feature(X, "u3", HF, t, True, False)
                    by_feature(X, "w3", AF, t, False, True).then_inc(S["fill_x"], 1)
                    yield
                    yield
                for t in range(KT):
                    pe.wait_ge(S["tr"], at("tr", g, 2 * s + t + 1))
                    by_feature(Y, "w5", AF, t, True, False)
                    yield
                for t in range(KT):
                    pe.wait_ge(S["rh_hi"], at("rh_hi", g, 2 * s + 2))
                    pe.wait_ge(S["rh_lo"], at("rh_lo", g, 2 * s + 2))
                    by_feature(Y, "u5", RH, t, False, True).then_inc(S["fill_y"], 1)
                    yield
                yield
                pe.wait_ge(S["hf_new"], at("hf_new", g, 2 * s + 2))
                pe.wait_ge(S["tz"], at("tz", g, 2 * s + 2))
                for j in range(2):
                    to_nodes(X, hF, j).then_inc(S["fill_x"], 1)
                yield
            yield

        def pe_b(pe, g):
            later = has_before(g)
            XF, OF = (xf_hi, xf_lo), (of_hi, of_lo)
            for L in range(2):
                q, k, v, o = (("q2", "k2", "v2", "o2"), ("q3", "k3", "v3", "o3"))[L]
                src = (x2, x3)[L]
                if L == 0:
                    pe.wait_ge(S["a_ln"], at("a_ln", g, 8))
                    if later:
                        pe.wait_ge(S["s_min"], at("s_min", g, 0))
                    if later:
                        pe.wait_ge(S["res_b"], at("res_b", g, 0))
                    if later:
                        pe.wait_ge(S["pt_lo"], at("pt_lo", g, 0))
                else:
                    pe.wait_ge(S["b_ln"], at("b_ln", g, 4))
                for t in range(KT):
                    to_features(SB, src, t).then_inc(S["xf_fill"], 1)
                yield
                pe.wait_ge(S["xf_hi"], at("xf_hi", g, 2 * L + 2))
                pe.wait_ge(S["xf_lo"], at("xf_lo", g, 2 * L + 2))
                if L == 1:
                    pe.wait_ge(S["res_b"], at("res_b", g, 2))
                for t in range(KT):
                    by_feature((PTB, OB), q, XF, t, True, True).then_inc(S["qk_fill"], 1)
                    yield
                for t in range(KT):
                    by_feature(SB, k, XF, t, True, True).then_inc(S["qk_fill"], 1)
                    yield
                pe.wait_ge(S["q_lo"], at("q_lo", g, 2 * L + 2))
                for j in range(2):
                    by_node((PTB, OB), v, XF, j).then_inc(S["v_fill"], 1)
                    yield
                u0 = UNITS * L

                def scores(u):
                    if u >= UNITS:
                        return
                    if u < 2:
                        pe.wait_ge(S["k_lo"], at("k_lo", g, 2 * L + 2))
                        pe.wait_ge(S["stack"], at("stack", g, (L + 1) * 24 * 16))
                    else:
                        pe.wait_ge(S["s_min"], at("s_min", g, 2 * (u0 + u - 1)))
                    r, b = u // 4, u // 4 // KT
                    for j in range(2):
                        h = 2 * (u % 4) + j
                        last = nc.tensor.matmul(SB[u % 2][:, j * N:(j + 1) * N],
                                                qs[:, h, r * P:(r + 1) * P], ks[:, h, b * N:(b + 1) * N],
                                                start=True, stop=True)
                    last.then_inc(S["s_fill"], 1)

                def transposes(u):
                    pe.wait_ge(S["p_exp"], at("p_exp", g, 2 * (u0 + u + 1)))
                    if u == 0:
                        pe.wait_ge(S["v_lo"], at("v_lo", g, 2 * L + 2))
                    else:
                        pe.wait_ge(S["pt_lo"], at("pt_lo", g, u0 + u))
                    for j in range(2):
                        for c in range(KT):
                            i = j * KT + c
                            last = nc.tensor.transpose(PTB[:, i * P:(i + 1) * P],
                                                       p_sb[:, u % 2, j, c * P:(c + 1) * P], ident[:, :])
                    last.then_inc(S["pt_fill"], 1)

                def weighted_sum(u):
                    pe.wait_ge(S["pt_hi"], at("pt_hi", g, u0 + u + 1))
                    pe.wait_ge(S["pt_lo"], at("pt_lo", g, u0 + u + 1))
                    r, b = u // 4, u // 4 // KT
                    if u % 4 == 0 and u > 0:
                        pe.wait_ge(S["norm"], at("norm", g, RT * L + r))
                    for j in range(2):
                        h = 2 * (u % 4) + j
                        o_ = OB[:, h * (HD + 1):(h + 1) * (HD + 1)]
                        for c in range(KT):
                            i = j * KT + c
                            ph = pt_hi[:, u % 2, i * P:(i + 1) * P]
                            pl = pt_lo[:, u % 2, i * P:(i + 1) * P]
                            vr = b * KT + c
                            nc.tensor.matmul(o_, ph, v_hi[:, vr, h, 0:HD + 1], start=c == 0, stop=False)
                            nc.tensor.matmul(o_[:, 0:HD], ph, v_lo[:, vr, h, :], start=False, stop=False)
                            last = nc.tensor.matmul(o_, pl, v_hi[:, vr, h, 0:HD + 1], start=False, stop=c == KT - 1)
                    last.then_inc(S["pv"], 1)

                scores(0)
                yield
                for u in range(UNITS):
                    scores(u + 1)
                    transposes(u)
                    if u:
                        weighted_sum(u - 1)
                    yield
                weighted_sum(UNITS - 1)
                yield
                pe.wait_ge(S["norm"], at("norm", g, RT * (L + 1)))
                for t in range(KT):
                    to_features(SB, oN, t).then_inc(S["of_fill"], 1)
                yield
                pe.wait_ge(S["of_hi"], at("of_hi", g, 2 * L + 2))
                pe.wait_ge(S["of_lo"], at("of_lo", g, 2 * L + 2))
                for j in range(2):
                    by_node((PTB, OB), o, OF, j).then_inc(S["o_fill"], 1)
                    yield
            yield

        def act_a(act, g):
            later = has_before(g)
            A = nc.scalar.activation
            act.wait_ge(S["x_loaded"], at("x_loaded", g, 16))
            if later:
                act.wait_ge(S["fill_x"], at("fill_x", g, -2))
            for j in range(2):
                A(hn_hi[:, 2 * j:2 * j + 2, :], xin[:, 2 * j:2 * j + 2, :], ACT.Copy).then_inc(S["hn_hi"], 1)
            for t in range(KT):
                act.wait_ge(S["fill_x"], at("fill_x", g, t + 1))
                if t == 0:
                    if later:
                        act.wait_ge(S["fill_y"], at("fill_y", g, 0))
                A(af_hi[:, t, :], X[t][:, :], ACT.Copy).then_inc(S["af_hi"], 1)
                yield
            yield
            yield
            act.wait_ge(S["a_ln"], at("a_ln", g, 4))
            act.wait_ge(S["fill_x"], at("fill_x", g, 2))
            for j in range(2):
                A(hn_hi[:, 2 * j:2 * j + 2, :], x1[:, 2 * j:2 * j + 2, :], ACT.Copy).then_inc(S["hn_hi"], 1)
            for t in range(KT):
                act.wait_ge(S["fill_x"], at("fill_x", g, 2 + t + 1))
                A(hf_hi[:, t, :], X[t][:, :], ACT.Copy).then_inc(S["hf_hi"], 1)
                A(hF[:, t, :], X[t][:, :], ACT.Copy).then_inc(S["hf32"], 1)
            yield
            for s in range(STEPS):
                fx = 4 + 6 * s
                for t in range(KT):
                    act.wait_ge(S["fill_x"], at("fill_x", g, fx + t + 1))
                    act.wait_ge(S["fill_y"], at("fill_y", g, 2 + 4 * s))
                    A(af_hi[:, t, :], X[t][:, :], ACT.Copy).then_inc(S["af_hi"], 1)
                    yield
                yield
                yield
                for t in range(KT):
                    act.wait_ge(S["fill_y"], at("fill_y", g, 2 + 4 * s + t + 1))
                    if later or 2 * s > 0:
                        act.wait_ge(S["rh"], at("rh", g, 2 * s))
                    A(trb[:, t, :], Y[t][:, :], ACT.Tanh, bias=bias[:, 1, t:t + 1], scale=0.5 / WS).then_inc(S["tr"], 1)
                    yield
                for t in range(KT):
                    act.wait_ge(S["fill_x"], at("fill_x", g, fx + 2 + t + 1))
                    if later or 2 * s > 0:
                        act.wait_ge(S["upd"], at("upd", g, 2 * s))
                    A(tzb[:, t, :], X[t][:, :], ACT.Tanh, bias=bias[:, 0, t:t + 1], scale=0.5 / WS).then_inc(S["tz"], 1)
                    yield
                    act.wait_ge(S["rh"], at("rh", g, 2 * s + t + 1))
                    act.wait_ge(S["fill_y"], at("fill_y", g, 2 + 4 * s))
                    A(rh_hi[:, t, :], rhb[:, t, :], ACT.Copy).then_inc(S["rh_hi"], 1)
                    yield
                yield
                yield
                for t in range(KT):
                    act.wait_ge(S["fill_y"], at("fill_y", g, 4 + 4 * s + t + 1))
                    if later or 2 * s > 0:
                        act.wait_ge(S["dif"], at("dif", g, 2 * s))
                    A(tvb[:, t, :], Y[t][:, :], ACT.Tanh, bias=bias[:, 2, t:t + 1], scale=1.0 / WS).then_inc(S["tv"], 1)
                    yield
                if s < STEPS - 1:
                    for t in range(KT):
                        act.wait_ge(S["hf_new"], at("hf_new", g, 2 * s + t + 1))
                        A(hf_hi[:, t, :], hF[:, t, :], ACT.Copy).then_inc(S["hf_hi"], 1)
                yield
                if s < STEPS - 1:
                    for j in range(2):
                        act.wait_ge(S["fill_x"], at("fill_x", g, fx + 4 + j + 1))
                        A(hn_hi[:, 2 * j:2 * j + 2, :], X[j][:, :].rearrange("p (a b) -> p a b", a=2), ACT.Copy).then_inc(S["hn_hi"], 1)
                yield
            yield

        def act_b(act, g):
            later = has_before(g)
            A = nc.scalar.activation
            for L in range(2):
                if later or 2 * L > 0:
                    act.wait_ge(S["v_fill"], at("v_fill", g, 2 * L))
                for t in range(KT):
                    act.wait_ge(S["xf_fill"], at("xf_fill", g, 2 * L + t + 1))
                    A(xf_hi[:, t, :], SB[t][:, :], ACT.Copy).then_inc(S["xf_hi"], 1)
                yield
                for name, m, buf in (("q_hi", 3, q_hi), ("k_hi", 4, k_hi)):
                    if later or L * 24 * 16 > 0:
                        act.wait_ge(S["stack"], at("stack", g, L * 24 * 16))
                    for t in range(KT):
                        act.wait_ge(S["qk_fill"], at("qk_fill", g, 4 * L + 2 * (m - 3) + t + 1))
                        if L == 0:
                            A(buf[:, t, :], (SB if m == 4 else (PTB, OB))[t][:, :], ACT.Identity, bias=bias[:, m, t:t + 1], scale=1.0).then_inc(S[name], 1)
                        else:
                            A(buf[:, t, :], (SB if m == 4 else (PTB, OB))[t][:, :], ACT.Copy).then_inc(S[name], 1)
                        yield
                if later or L * UNITS > 0:
                    act.wait_ge(S["pv"], at("pv", g, L * UNITS))
                for j in range(2):
                    act.wait_ge(S["v_fill"], at("v_fill", g, 2 * L + j + 1))
                    A(v_hi[:, 2 * j:2 * j + 2, :, 0:HD].rearrange("p a h d -> p (a h) d"),
                      (PTB, OB)[j][:, :].rearrange("p (h d) -> p h d", d=HD), ACT.Copy, scale=1.0 / WS).then_inc(S["v_hi"], 1)
                    yield
                u0 = UNITS * L

                def exps(u):
                    if u >= UNITS:
                        return
                    if later or u0 + u - 1 > 0:
                        act.wait_ge(S["pt_fill"], at("pt_fill", g, u0 + u - 1))
                    for j in range(2):
                        act.wait_ge(S["s_min"], at("s_min", g, 2 * (u0 + u) + j + 1))
                        A(p_sb[:, u % 2, j, :], sp[:, u % 3, j, :], ACT.Exp, bias=s_min[:, u % 3, j:j + 1], scale=-1.0).then_inc(S["p_exp"], 1)

                exps(0)
                yield
                for u in range(UNITS):
                    act.wait_ge(S["pt_fill"], at("pt_fill", g, u0 + u + 1))
                    if later or u0 + u - 1 > 0:
                        act.wait_ge(S["pv"], at("pv", g, u0 + u - 1))
                    A(pt_hi[:, u % 2, :], PTB[:, :], ACT.Copy).then_inc(S["pt_hi"], 1)
                    exps(u + 1)
                    yield
                yield
                if later or 2 * L > 0:
                    act.wait_ge(S["o_fill"], at("o_fill", g, 2 * L))
                for t in range(KT):
                    act.wait_ge(S["of_fill"], at("of_fill", g, 2 * L + t + 1))
                    if L == 0:
                        A(of_hi[:, t, :], SB[t][:, :], ACT.Identity, bias=bias_in[:, 7, t:t + 1], scale=1.0).then_inc(S["of_hi"], 1)
                    else:
                        A(of_hi[:, t, :], SB[t][:, :], ACT.Copy).then_inc(S["of_hi"], 1)
                yield
                yield
                yield
            yield

        V = nc.vector

        def stats(dve, src, st, mv, names, g, n):
            later = has_before(g)
            s_st, s_mv, s_ve = names
            if later or RT * n > 0:
                dve.wait_ge(S[s_mv], at(s_mv, g, RT * n))
            for r in range(RT):
                V.bn_stats(st[:, r, :], src[:, r, :]).then_inc(S[s_st], 1)
            dve.wait_ge(S[s_st], at(s_st, g, RT * (n + 1)))
            settled(dve)
            for r in range(RT):
                V.bn_aggr(mv[:, r, :], st[:, r, :]).then_inc(S[s_mv], 1)

        def normalise(dve, dst, src, mv, rs, names, g, n):
            later = has_before(g)
            s_rs, s_ln = names
            dve.wait_ge(S[s_rs], at(s_rs, g, n + 1))
            for r in range(RT):
                V.tensor_scalar(dst[:, r, :], src[:, r, :], mv[:, r, 0:1], rs[:, r:r + 1],
                                ALU.subtract, ALU.mult).then_inc(S[s_ln], 1)

        def low_part(dve, name, lo, src, hi):
            V.tensor_tensor(lo, src, hi, ALU.subtract).then_inc(S[name], 1)

        def dve_a(dve, g):
            later = has_before(g)
            if later:
                dve.wait_ge(S["fill_x"], at("fill_x", g, -2))
            dve.wait_ge(S["x_loaded"], at("x_loaded", g, 16))
            for j in range(2):
                dve.wait_ge(S["hn_hi"], at("hn_hi", g, j + 1))
                low_part(dve, "hn_lo", hn_lo[:, 2 * j:2 * j + 2, :], xin[:, 2 * j:2 * j + 2, :], hn_hi[:, 2 * j:2 * j + 2, :])
            if later:
                dve.wait_ge(S["fill_y"], at("fill_y", g, 0))
            for t in range(KT):
                dve.wait_ge(S["af_hi"], at("af_hi", g, t + 1))
                low_part(dve, "af_lo", af_lo[:, t, :], X[t][:, :], af_hi[:, t, :])
                yield
            dve.wait_ge(S["xb"], at("xb", g, 1))
            if later:
                dve.wait_ge(S["a_ln"], at("a_ln", g, 0))
            for j in range(2):
                dve.wait_ge(S["fill_y"], at("fill_y", g, j + 1))
                V.scalar_tensor_tensor(out=tA[:, 2 * j:2 * j + 2, :].rearrange("p a b -> p (a b)"), in0=Y[j][:, :], scalar=1.0 / WS,
                                       in1=xb[:, 2 * j:2 * j + 2, :].rearrange("p a b -> p (a b)"),
                                       op0=ALU.mult, op1=ALU.add).then_inc(S["res_a"], 1)
                if j == 1:
                    dve.wait_ge(S["res_a"], at("res_a", g, 2))
                    stats(dve, tA, stA, mvA, ("a_st", "a_mv", "a_ve"), g, 0)
                    if later:
                        dve.wait_ge(S["res_a"], at("res_a", g, 0))
                    normalise(dve, x1, tA, mvA, rsA, ("a_rs", "a_ln"), g, 0)
                yield
            for j in range(2):
                dve.wait_ge(S["hn_hi"], at("hn_hi", g, 2 + j + 1))
                low_part(dve, "hn_lo", hn_lo[:, 2 * j:2 * j + 2, :], x1[:, 2 * j:2 * j + 2, :], hn_hi[:, 2 * j:2 * j + 2, :])
            for t in range(KT):
                dve.wait_ge(S["hf32"], at("hf32", g, t + 1))
                low_part(dve, "hf_lo", hf_lo[:, t, :], X[t][:, :], hf_hi[:, t, :])
            yield
            for s in range(STEPS):
                fx = 4 + 6 * s
                dve.wait_ge(S["fill_y"], at("fill_y", g, 2 + 4 * s))
                for t in range(KT):
                    dve.wait_ge(S["af_hi"], at("af_hi", g, 2 + 2 * s + t + 1))
                    low_part(dve, "af_lo", af_lo[:, t, :], X[t][:, :], af_hi[:, t, :])
                    yield
                yield
                yield
                if later or 2 * s > 0:
                    dve.wait_ge(S["rh_lo"], at("rh_lo", g, 2 * s))
                if later or 2 * s > 0:
                    dve.wait_ge(S["rh_hi"], at("rh_hi", g, 2 * s))
                for t in range(KT):
                    dve.wait_ge(S["tr"], at("tr", g, 2 * s + t + 1))
                    if s == 0:
                        dve.wait_ge(S["hf32"], at("hf32", g, t + 1))
                    V.scalar_tensor_tensor(out=rhb[:, t, :], in0=trb[:, t, :], scalar=1.0, in1=hF[:, t, :],
                                           op0=ALU.add, op1=ALU.mult).then_inc(S["rh"], 1)
                    yield
                for t in range(KT):
                    yield
                    dve.wait_ge(S["rh_hi"], at("rh_hi", g, 2 * s + t + 1))
                    low_part(dve, "rh_lo", rh_lo[:, t, :], rhb[:, t, :], rh_hi[:, t, :])
                    yield
                yield
                yield
                for t in range(KT):
                    dve.wait_ge(S["tv"], at("tv", g, 2 * s + t + 1))
                    if later or 2 * s + t > 0:
                        dve.wait_ge(S["upd"], at("upd", g, 2 * s + t))
                    V.tensor_tensor(difb[:, t, :], tvb[:, t, :], hF[:, t, :], ALU.subtract).then_inc(S["dif"], 1)
                    dve.wait_ge(S["dif"], at("dif", g, 2 * s + t + 1))
                    dve.wait_ge(S["tz"], at("tz", g, 2 * s + t + 1))
                    if later or 2 * s + t > 0:
                        dve.wait_ge(S["hf_new"], at("hf_new", g, 2 * s + t))
                    V.scalar_tensor_tensor(out=updb[:, t, :], in0=tzb[:, t, :], scalar=1.0, in1=difb[:, t, :],
                                           op0=ALU.add, op1=ALU.mult).then_inc(S["upd"], 1)
                    dve.wait_ge(S["upd"], at("upd", g, 2 * s + t + 1))
                    V.scalar_tensor_tensor(out=hF[:, t, :], in0=updb[:, t, :], scalar=0.5, in1=hF[:, t, :],
                                           op0=ALU.mult, op1=ALU.add).then_inc(S["hf_new"], 1)
                    yield
                yield
                if s < STEPS - 1:
                    for t in range(KT):
                        dve.wait_ge(S["hf_hi"], at("hf_hi", g, 2 + 2 * s + t + 1))
                        low_part(dve, "hf_lo", hf_lo[:, t, :], hF[:, t, :], hf_hi[:, t, :])
                    for j in range(2):
                        dve.wait_ge(S["hn_hi"], at("hn_hi", g, 4 + 2 * s + j + 1))
                        low_part(dve, "hn_lo", hn_lo[:, 2 * j:2 * j + 2, :].rearrange("p a b -> p (a b)"), X[j][:, :],
                                 hn_hi[:, 2 * j:2 * j + 2, :].rearrange("p a b -> p (a b)"))
                else:
                    for j in range(2):
                        dve.wait_ge(S["fill_x"], at("fill_x", g, fx + 4 + j + 1))
                        V.tensor_tensor(tA[:, 2 * j:2 * j + 2, :].rearrange("p a b -> p (a b)"), X[j][:, :],
                                        x1[:, 2 * j:2 * j + 2, :].rearrange("p a b -> p (a b)"), ALU.add).then_inc(S["res_a"], 1)
                    dve.wait_ge(S["res_a"], at("res_a", g, 4))
                    stats(dve, tA, stA, mvA, ("a_st", "a_mv", "a_ve"), g, 1)
                    if later:
                        dve.wait_ge(S["xb2"], at("xb2", g, 0))
                    if later:
                        dve.wait_ge(S["xf_fill"], at("xf_fill", g, -2))
                    normalise(dve, x2, tA, mvA, rsA, ("a_rs", "a_ln"), g, 1)
                yield
            yield

        def dve_b(dve, g):
            later = has_before(g)
            for L in range(2):
                if later or 2 * L > 0:
                    dve.wait_ge(S["v_fill"], at("v_fill", g, 2 * L))
                for t in range(KT):
                    dve.wait_ge(S["xf_hi"], at("xf_hi", g, 2 * L + t + 1))
                    low_part(dve, "xf_lo", xf_lo[:, t, :], SB[t][:, :], xf_hi[:, t, :])
                yield
                if later or L * 24 * 16 > 0:
                    dve.wait_ge(S["stack"], at("stack", g, L * 24 * 16))
                for i, (hi, lo, his, los) in enumerate(((q_hi, q_lo, "q_hi", "q_lo"), (k_hi, k_lo, "k_hi", "k_lo"))):
                    bank = (SB if i else (PTB, OB))
                    for t in range(KT):
                        dve.wait_ge(S[his], at(his, g, 2 * L + t + 1))
                        if L == 0:
                            V.scalar_tensor_tensor(out=lo[:, t, :], in0=bank[t][:, :], scalar=bias[:, 3 + i, t:t + 1],
                                                   in1=hi[:, t, :], op0=ALU.add, op1=ALU.subtract).then_inc(S[los], 1)
                        else:
                            low_part(dve, los, lo[:, t, :], bank[t][:, :], hi[:, t, :])
                        yield
                if later or L * UNITS > 0:
                    dve.wait_ge(S["pv"], at("pv", g, L * UNITS))
                for j in range(2):
                    dve.wait_ge(S["v_hi"], at("v_hi", g, 2 * L + j + 1))
                    V.scalar_tensor_tensor(out=v_lo[:, 2 * j:2 * j + 2, :, :].rearrange("p a h d -> p (a h) d"),
                                           in0=(PTB, OB)[j][:, :].rearrange("p (h d) -> p h d", d=HD), scalar=1.0 / WS,
                                           in1=v_hi[:, 2 * j:2 * j + 2, :, 0:HD].rearrange("p a h d -> p (a h) d"),
                                           op0=ALU.mult, op1=ALU.subtract).then_inc(S["v_lo"], 1)
                    yield
                u0 = UNITS * L

                def masked(u):
                    if u >= UNITS:
                        return
                    dve.wait_ge(S["s_fill"], at("s_fill", g, u0 + u + 1))
                    if later or 2 * (u0 + u - 2) > 0:
                        dve.wait_ge(S["p_exp"], at("p_exp", g, 2 * (u0 + u - 2)))
                    settled(dve)
                    qt = (u // 4) % KT
                    for j in range(2):
                        V.tensor_tensor_reduce(out=sp[:, u % 3, j, :], in0=SB[u % 2][:, j * N:(j + 1) * N],
                                               in1=neg_mask[:, L, qt, :], scale=1.0 / (WS * WS), scalar=3.0e38,
                                               op0=ALU.add, op1=ALU.min,
                                               accum_out=s_min[:, u % 3, j:j + 1]).then_inc(S["s_min"], 1)

                def normalise_heads(r):
                    n = RT * L + r
                    o_ = OB[:, 0:H * (HD + 1)].rearrange("p (h d) -> p h d", d=HD + 1)
                    if later or n - 1 > 0:
                        dve.wait_ge(S["norm"], at("norm", g, n - 1))
                    V.reciprocal(rec[:, r % 2, :], o_[:, :, HD]).then_inc(S["rec"], 1)
                    dve.wait_ge(S["rec"], at("rec", g, n + 1))
                    if r == 0:
                        if later or 2 * L > 0:
                            dve.wait_ge(S["of_fill"], at("of_fill", g, 2 * L))
                    V.tensor_tensor(oN[:, r, :].rearrange("p (h d) -> p h d", d=HD), o_[:, :, 0:HD],
                                    rec[:, r % 2, :].unsqueeze(2).to_broadcast([P, H, HD]), ALU.mult).then_inc(S["norm"], 1)

                masked(0)
                yield
                for u in range(UNITS):
                    masked(u + 1)
                    if u % 4 == 0 and u > 0:
                        dve.wait_ge(S["pv"], at("pv", g, u0 + u))
                        normalise_heads(u // 4 - 1)
                    dve.wait_ge(S["pt_hi"], at("pt_hi", g, u0 + u + 1))
                    if later or u0 + u - 1 > 0:
                        dve.wait_ge(S["pv"], at("pv", g, u0 + u - 1))
                    low_part(dve, "pt_lo", pt_lo[:, u % 2, :], PTB[:, :], pt_hi[:, u % 2, :])
                    yield
                dve.wait_ge(S["pv"], at("pv", g, u0 + UNITS))
                normalise_heads(RT - 1)
                yield
                if later or 2 * L > 0:
                    dve.wait_ge(S["o_fill"], at("o_fill", g, 2 * L))
                for t in range(KT):
                    dve.wait_ge(S["of_hi"], at("of_hi", g, 2 * L + t + 1))
                    if L == 0:
                        V.scalar_tensor_tensor(out=of_lo[:, t, :], in0=SB[t][:, :], scalar=bias_in[:, 7, t:t + 1],
                                               in1=of_hi[:, t, :], op0=ALU.add, op1=ALU.subtract).then_inc(S["of_lo"], 1)
                    else:
                        low_part(dve, "of_lo", of_lo[:, t, :], SB[t][:, :], of_hi[:, t, :])
                yield
                if L == 0:
                    dve.wait_ge(S["xb2"], at("xb2", g, 1))
                    if later:
                        dve.wait_ge(S["b_ln"], at("b_ln", g, 0))
                else:
                    dve.wait_ge(S["b_ln"], at("b_ln", g, 4))
                if later:
                    dve.wait_ge(S["obe"], at("obe", g, 0))
                for j in range(2):
                    dve.wait_ge(S["o_fill"], at("o_fill", g, 2 * L + j + 1))
                    if L == 0:
                        V.scalar_tensor_tensor(out=tB[:, 2 * j:2 * j + 2, :].rearrange("p a b -> p (a b)"), in0=(PTB, OB)[j][:, :],
                                               scalar=1.0 / WS, in1=xb2[:, 2 * j:2 * j + 2, :].rearrange("p a b -> p (a b)"),
                                               op0=ALU.mult, op1=ALU.add).then_inc(S["res_b"], 1)
                    else:
                        V.scalar_tensor_tensor(out=tB[:, 2 * j:2 * j + 2, :], in0=(PTB, OB)[j][:, :].rearrange("p (a b) -> p a b", a=2),
                                               scalar=1.0 / WS, in1=bp_r.unsqueeze(1).to_broadcast([P, 2, D]),
                                               op0=ALU.mult, op1=ALU.add).then_inc(S["res_b"], 1)
                    if j == 1:
                        dve.wait_ge(S["res_b"], at("res_b", g, 2 * L + 2))
                        names = ("b_st", "b_mv", "b_ve")
                        stats(dve, tB, stB, mvB, names, g, L)
                        if L == 0:
                            if later:
                                dve.wait_ge(S["xbe"], at("xbe", g, 0))
                            if later:
                                dve.wait_ge(S["xf_fill"], at("xf_fill", g, 0))
                            normalise(dve, x3, tB, mvB, rsB, ("b_rs", "b_ln"), g, 0)
                        else:
                            if later:
                                dve.wait_ge(S["gam"], at("gam", g, 0))
                            normalise(dve, o_n, tB, mvB, rsB, ("b_rs", "b_ln"), g, 1)
                            dve.wait_ge(S["gam"], at("gam", g, 1))
                            dve.wait_ge(S["obe"], at("obe", g, 1))
                            if later:
                                dve.wait_ge(S["b_ln"], at("b_ln", g, 0))
                            V.tensor_tensor(tF[:, :, :], o_g[:, :, :], obe[:, :, :], ALU.add).then_inc(S["t_fin"], 1)
                            dve.wait_ge(S["t_fin"], at("t_fin", g, 1))
                            stats(dve, tF, stB, mvB, names, g, 2)
                            if later:
                                dve.wait_ge(S["stored"], at("stored", g, 0))
                            normalise(dve, y_out, tF, mvB, rsB, ("b_rs", "b_ln"), g, 2)
                    yield
            yield

        G = nc.gpsimd

        def rstd(pool, mv, ve, rs, names, g, n):
            later = has_before(g)
            s_mv, s_ve, s_rs = names
            pool.wait_ge(S[s_mv], at(s_mv, g, RT * (n + 1)))
            if later or n > 0:
                pool.wait_ge(S[s_rs], at(s_rs, g, n))
            G.tensor_tensor(ve[:, :], mv[:, :, 1], eps_t[:, :], ALU.add).then_inc(S[s_ve], 1)
            pool.wait_ge(S[s_ve], at(s_ve, g, n + 1))
            G.tensor_tensor(rs[:, :], ve[:, :], m_half[:, :], ALU.pow).then_inc(S[s_rs], 1)

        def pool_a(pool, g):
            later = has_before(g)
            pool.wait_ge(S["x_loaded"], at("x_loaded", g, 16))
            if later:
                pool.wait_ge(S["res_a"], at("res_a", g, -2))
            G.tensor_tensor(xb[:, :, :], xin[:, :, :], b0_r.unsqueeze(1).to_broadcast([P, RT, D]), ALU.add).then_inc(S["xb"], 1)
            for _ in range(3):
                yield
            if later:
                pool.wait_ge(S["a_ln"], at("a_ln", g, 0))
            rstd(pool, mvA, veA, rsA, ("a_mv", "a_ve", "a_rs"), g, 0)
            yield
            yield
            for s in range(STEPS):
                for _ in range(16):
                    if s == STEPS - 1 and _ == 15:
                        pool.wait_ge(S["a_ln"], at("a_ln", g, 4))
                        rstd(pool, mvA, veA, rsA, ("a_mv", "a_ve", "a_rs"), g, 1)
                    yield
            yield

        def pool_b(pool, g):
            later = has_before(g)
            pool.wait_ge(S["a_ln"], at("a_ln", g, 8))
            if later:
                pool.wait_ge(S["res_b"], at("res_b", g, -2))
            G.tensor_tensor(xb2[:, :, :], x2[:, :, :], bo_r.unsqueeze(1).to_broadcast([P, RT, D]), ALU.add).then_inc(S["xb2"], 1)
            for i in range(B_SLOTS // 2 - 1):
                yield
            if later:
                pool.wait_ge(S["b_ln"], at("b_ln", g, 0))
            rstd(pool, mvB, veB, rsB, ("b_mv", "b_ve", "b_rs"), g, 0)
            yield
            pool.wait_ge(S["b_ln"], at("b_ln", g, 4))
            if later:
                pool.wait_ge(S["obe"], at("obe", g, 0))
            G.tensor_tensor(xbe[:, :, :], x3[:, :, :], bet_r.unsqueeze(1).to_broadcast([P, RT, D]), ALU.add).then_inc(S["xbe"], 1)
            for i in range(B_SLOTS // 2 - 1):
                yield
            rstd(pool, mvB, veB, rsB, ("b_mv", "b_ve", "b_rs"), g, 1)
            pool.wait_ge(S["res_b"], at("res_b", g, 4))
            if later:
                pool.wait_ge(S["t_fin"], at("t_fin", g, 0))
            pool.wait_ge(S["xbe"], at("xbe", g, 1))
            G.tensor_tensor(obe[:, :, :], xbe[:, :, :], tB[:, :, :], ALU.add).then_inc(S["obe"], 1)
            pool.wait_ge(S["b_ln"], at("b_ln", g, 8))
            G.tensor_tensor(o_g[:, :, :], o_n[:, :, :], gam_r.unsqueeze(1).to_broadcast([P, RT, D]), ALU.mult).then_inc(S["gam"], 1)
            rstd(pool, mvB, veB, rsB, ("b_mv", "b_ve", "b_rs"), g, 2)
            yield
            yield

        def load_x(sp_, g):
            later = has_before(g)
            if later:
                sp_.wait_ge(S["hn_hi"], at("hn_hi", g, -6))
            if later:
                sp_.wait_ge(S["hn_lo"], at("hn_lo", g, -6))
            if later:
                sp_.wait_ge(S["xb"], at("xb", g, 0))
            settled(sp_)
            sp_.dma_start(xin[:, :, :], x_v[g]).then_inc(S["x_loaded"], 16)

        def sp_a(sp_, g):
            later = has_before(g)
            for _ in range(A_SLOTS - 1):
                yield
            if not (isinstance(g, int) and g == GROUPS - 1):
                load_x(sp_, g + 1)
            yield

        def sp_b(sp_, g):
            later = has_before(g)
            for L in range(2):
                yield
                for dst, hi, lo, order, los in ((qs, q_hi, q_lo, "hhl", "q_lo"), (ks, k_hi, k_lo, "hlh", "k_lo")):
                    yield
                    sp_.wait_ge(S[los], at(los, g, 2 * L + 2))
                    for c, part in enumerate(order):
                        src = hi if part == "h" else lo
                        for q4 in range(4):
                            sp_.dma_start(dst[c * HD:(c + 1) * HD, q4:H:4, :],
                                          src[q4 * HD:(q4 + 1) * HD, :, :]).then_inc(S["stack"], 16)
                    yield
                for _ in range(B_SLOTS // 2 - 5):
                    yield
            sp_.wait_ge(S["b_ln"], at("b_ln", g, 12))
            settled(sp_)
            sp_.dma_start(out_v[g], y_out[:, :, :]).then_inc(S["stored"], 16)
            yield

        A_SLOTS = 5 + STEPS * 16 + 1
        B_SLOTS = 2 * (7 + 1 + UNITS + 1 + 3)

        def step(stream):
            next(stream, None)

        def merged(a, b):
            done = 0
            for i in range(B_SLOTS + 1):
                step(b)
                while done * (B_SLOTS + 1) < (i + 1) * A_SLOTS:
                    step(a)
                    done += 1

        def whole(eng, a_stream, b_stream):
            for _ in a_stream(eng, 0):
                pass
            merged(a_stream(eng, 1), b_stream(eng, 0))
            with eng.Fori(2, GROUPS - 1) as g:
                merged(a_stream(eng, g), b_stream(eng, g - 1))
            merged(a_stream(eng, GROUPS - 1), b_stream(eng, GROUPS - 2))
            for _ in b_stream(eng, GROUPS - 1):
                pass

        block = ctx.enter_context(nc.Block())

        @block.sync
        def _(sp_):
            load_x(sp_, 0)
            plain = [adjT, w0, w3T[0:D, :], w4T[0:D, :], w5T[0:D, :], u3T, u5T, wq, wk, wv, wo,
                     wqkv[:, 0:D], wqkv[:, D:2 * D], wqkv[:, 2 * D:3 * D], wproj]
            n = 0
            for i, m in enumerate(plain):
                sp_.dma_start(raw[:, i], rows(m)).then_inc(w_in, 16)
                n += 1
            for i, m in enumerate((w3T, w4T, w5T)):
                sp_.dma_start(raw2[:, i], rows(m[D:2 * D, :])).then_inc(w_in, 16)
                n += 1
            sp_.dma_start(adj_sb[:, :, :], rows(adj)).then_inc(w_in, 16)
            for i, v in enumerate((b0, bo, bproj, gamma, beta)):
                sp_.dma_start(rep[:, i, :], v.rearrange("(a n) -> a n", a=1).to_broadcast([P, D])).then_inc(w_in, 16)
            for i, v in enumerate((b3, b4, b5, bu3, bu5, bq, bk, bv)):
                sp_.dma_start(bias_in[:, i, :], v.rearrange("(t p) -> p t", p=P), allow_slow_non_contiguous=True).then_inc(w_in, 16)
            whole(sp_, sp_a, sp_b)
            sp_.wait_ge(S["stored"], GROUPS * 16)

        N_IN = 15 + 3 + 1 + 5 + 8

        @block.tensor
        def _(pe):
            pe.wait_ge(id_s, 2)
            pe.wait_ge(w_lo_s, len(MATS))
            pe.wait_ge(one_s, 1)
            whole(pe, pe_a, pe_b)

        @block.scalar
        def _(act):
            act.wait_ge(w_in, N_IN * 16)
            for i, m in enumerate(MATS):
                if m in ("w3", "w4", "w5"):
                    act.wait_ge(w_set, 3)
                nc.scalar.activation(W_hi[:, i], raw[:, i], ACT.Copy, scale=SCALE[m]).then_inc(w_hi_s, 1)
            act.wait_ge(masks_ready, 9)
            whole(act, act_a, act_b)

        @block.vector
        def _(dve):
            V.memset(v_hi[:, :, :, :], 1.0).then_inc(one_s, 1)
            dve.wait_ge(w_in, N_IN * 16)
            for i in range(3):
                V.tensor_tensor(raw[:, 2 + i], raw[:, 2 + i], raw2[:, i], ALU.add).then_inc(w_set, 1)
            dve.wait_ge(w_set, 3)
            for i, m in enumerate(MATS):
                dve.wait_ge(w_hi_s, i + 1)
                V.scalar_tensor_tensor(out=W_lo[:, i], in0=raw[:, i], scalar=SCALE[m], in1=W_hi[:, i],
                                       op0=ALU.mult, op1=ALU.subtract).then_inc(w_lo_s, 1)
            V.tensor_scalar(neg_mask[:, 0], adj_sb[:, :, :], -1.0, 1.0, ALU.mult, ALU.add).then_inc(masks_ready, 1)
            V.tensor_scalar(neg_mask[:, 1], adj_sb[:, :, :], 0.0, MASK_L3, ALU.is_equal, ALU.mult).then_inc(masks_ready, 1)
            V.tensor_tensor(bias[:, 0, :], bias_in[:, 0, :], bias_in[:, 3, :], ALU.add).then_inc(masks_ready, 1)
            V.tensor_tensor(bias[:, 1, :], bias_in[:, 1, :], bias_in[:, 3, :], ALU.add).then_inc(masks_ready, 1)
            V.tensor_tensor(bias[:, 2, :], bias_in[:, 2, :], bias_in[:, 4, :], ALU.add).then_inc(masks_ready, 1)
            V.tensor_scalar(bias[:, 3, :], bias_in[:, 5, :], -WS * QK, None, ALU.mult).then_inc(masks_ready, 1)
            V.tensor_scalar(bias[:, 4, :], bias_in[:, 6, :], WS, None, ALU.mult).then_inc(masks_ready, 1)
            dve.wait_ge(masks_ready, 7)
            V.tensor_scalar(neg_mask[:, 0], neg_mask[:, 0], MASK_L2 * WS * WS, None, ALU.mult).then_inc(masks_ready, 1)
            V.tensor_scalar(bias[:, 0:2, :], bias[:, 0:2, :], 0.5, None, ALU.mult).then_inc(masks_ready, 1)
            dve.wait_ge(masks_ready, 9)
            dve.wait_ge(one_s, 1)
            whole(dve, dve_a, dve_b)

        @block.gpsimd
        def _(pool):
            G.memset(ident[:, :], 0.0).then_inc(id_s, 1)
            G.memset(m_half[:, :], -0.5).then_inc(half_s, 1)
            G.memset(eps_t[:, :], EPS).then_inc(half_s, 1)
            pool.wait_ge(id_s, 1)
            G.affine_select(out=ident[:, :], in_=ident[:, :], compare_op=ALU.not_equal, fill=1.0, base=0,
                            pattern=[[-1, P]], channel_multiplier=1).then_inc(id_s, 1)
            pool.wait_ge(half_s, 2)
            pool.wait_ge(w_in, N_IN * 16)
            whole(pool, pool_a, pool_b)


def kernel(**inputs):
    import numpy as np
    import concourse.bacc as bacc
    from concourse import mybir as _mybir
    from concourse.bass_utils import run_bass_kernel_spmd

    def a(name):
        return np.ascontiguousarray(inputs[name])

    def t(name):
        return np.ascontiguousarray(np.asarray(inputs[name]).T)

    arrays = dict(
        x=a("x").reshape(B * N, D), adj=a("adj"), adjT=t("adj"), w0=a("L0_gnn_weight"), b0=a("L0_gnn_bias"),
        w3T=t("L1_gnn_w3_w"), b3=a("L1_gnn_w3_b"), u3T=t("L1_gnn_u3_w"), bu3=a("L1_gnn_u3_b"),
        w4T=t("L1_gnn_w4_w"), b4=a("L1_gnn_w4_b"), w5T=t("L1_gnn_w5_w"), b5=a("L1_gnn_w5_b"),
        u5T=t("L1_gnn_u5_w"), bu5=a("L1_gnn_u5_b"),
        wq=a("L2_gnn_Wq"), bq=a("L2_gnn_bq"), wk=a("L2_gnn_Wk"), bk=a("L2_gnn_bk"),
        wv=a("L2_gnn_Wv"), bv=a("L2_gnn_bv"), wo=a("L2_gnn_Wo"), bo=a("L2_gnn_bo"),
        wqkv=a("L3_gnn_w_qkv"), wproj=a("L3_gnn_w_proj"), bproj=a("L3_gnn_b_proj"),
        gamma=a("L3_gnn_ln_gamma"), beta=a("L3_gnn_ln_beta"))
    nc = bacc.Bacc("TRN2", target_bir_lowering=False, num_devices=1)
    args = [nc.dram_tensor(f"in_{n}", v.shape, _mybir.dt.from_np(v.dtype), kind="ExternalInput").ap() for n, v in arrays.items()]
    args.append(nc.dram_tensor("out", (B * N, D), _mybir.dt.float32, kind="ExternalOutput").ap())
    gnn_stack_kernel(nc, *args)
    r = run_bass_kernel_spmd(nc, [{f"in_{n}": v for n, v in arrays.items()}], core_ids=[0])
    return r.results[0]["out"].reshape(B, N, D)
```

```python
import concourse.bass as bass
from concourse import mybir
from contextlib import ExitStack
import math

B, N, D, H = 32, 256, 256, 8
HD = D // H
P = 128
GRAPHS = 2
COLS = GRAPHS * N
GROUPS = B // GRAPHS
RT = COLS // P
KT = D // P
STEPS = 3
UNITS = RT * H // 2
EPS = 1e-5
WS = 64.0
QK = 1.0 / math.sqrt(HD)
MASK_L2 = 1e9
MASK_L3 = 3.0e38

PER = dict(
    x_loaded=16, xb=1, xn_hi=2, xn_lo=2, hn_hi=6, hn_lo=6, fill_x=22, fill_y=14, af_hi=8, af_lo=8, res_a=4,
    hf32=2, hf_hi=6, hf_lo=6, tr=6, tz=6, tv=6, rh=6, rh_hi=6, rh_lo=6, z=6, zh=6, keep=6, zv=6, hf_new=6,
    a_st=8, a_mv=8, a_ve=2, a_rs=2, a_ln=8,
    xb2=1, xf_fill=4, xf_hi=4, xf_lo=4, qk_fill=8, q_hi=4, q_lo=4, k_hi=4, k_lo=4,
    v_fill=4, v_hi=4, v_lo=4, stack1=2 * 12 * 16, stack2=2 * 12 * 16, s_fill=2 * UNITS, s_min=4 * UNITS, p_exp=4 * UNITS, pt_fill=2 * UNITS,
    pt_hi=2 * UNITS, pt_lo=2 * UNITS, pv=2 * UNITS, rec=8, norm=8, of_fill=4, of_hi=4, of_lo=4, o_fill=4, res_b=4,
    gam=1, xbe=1, obe=1, t_fin=1,
    b_st=12, b_mv=12, b_ve=3, b_rs=3, b_ln=12, stored=16,
)

MATS = ["adjT", "w0", "w3", "w4", "w5", "u3", "u5", "q2", "k2", "v2", "o2", "q3", "k3", "v3", "o3"]
SCALE = {m: WS for m in MATS}
SCALE.update(adjT=1.0, u5=WS / 2, q2=-WS * QK, q3=-WS * QK)


def gnn_stack_kernel(nc, x, adj, adjT, w0, b0, w3T, b3, u3T, bu3, w4T, b4, w5T, b5, u5T, bu5,
                     wq, bq, wk, bk, wv, bv, wo, bo, wqkv, wproj, bproj, gamma, beta, out):
    f32, f16 = mybir.dt.float32, mybir.dt.float16
    ALU = mybir.AluOpType
    ACT = mybir.ActivationFunctionType

    x_v = x.rearrange("(g t p) d -> g p t d", t=RT, p=P)
    out_v = out.rearrange("(g t p) d -> g p t d", t=RT, p=P)

    def rows(m):
        return m.rearrange("(t p) n -> p t n", p=P)

    ctx = ExitStack()
    with ctx:
        def sb(name, shape, dt=f32):
            return ctx.enter_context(nc.sbuf_tensor(name, shape, dt))

        def sem(name):
            return ctx.enter_context(nc.semaphore(name))

        W_hi = sb("W_hi", [P, len(MATS), KT, D], f16)
        W_lo = sb("W_lo", [P, len(MATS), KT, D], f16)
        bufs = sb("bufs", [P, 10, RT, D])
        x3, tB, o_n, o_g, xbe, obe, tF, y_out, xb2, oN = (bufs[:, i] for i in range(10))
        raw = bufs[:, 0:8].rearrange("p s (m k) d -> p (s m) k d", k=KT)
        raw2 = bufs[:, 8:10].rearrange("p s (m k) d -> p (s m) k d", k=KT)
        adj_sb = sb("adj_sb", [P, KT, N])
        neg_mask = sb("neg_mask", [P, 2, KT, N])
        rep = sb("rep", [P, 5, D])
        b0_r, bo_r, bp_r, gam_r, bet_r = (rep[:, i, :] for i in range(5))
        bias_in = sb("bias_in", [P, 8, KT])
        bias = sb("bias", [P, 5, KT])
        ident = sb("ident", [P, P])
        m_half = sb("m_half", [P, RT])
        eps_t = sb("eps_t", [P, RT])
        xin = sb("xin", [P, RT, D])
        xb = sb("xb", [P, RT, D])
        xn_hi = sb("xn_hi", [P, RT, D], f16)
        xn_lo = sb("xn_lo", [P, RT, D], f16)
        hn_hi = sb("hn_hi", [P, RT, D], f16)
        hn_lo = sb("hn_lo", [P, RT, D], f16)
        af_hi = sb("af_hi", [P, KT, COLS], f16)
        af_lo = sb("af_lo", [P, KT, COLS], f16)
        hF = sb("hF", [P, KT, COLS])
        hf_hi = sb("hf_hi", [P, KT, COLS], f16)
        hf_lo = sb("hf_lo", [P, KT, COLS], f16)
        trb = sb("trb", [P, KT, COLS])
        tzb = sb("tzb", [P, KT, COLS])
        tvb = sb("tvb", [P, KT, COLS])
        rhb = sb("rhb", [P, KT, COLS])
        rh_hi = sb("rh_hi", [P, KT, COLS], f16)
        rh_lo = sb("rh_lo", [P, KT, COLS], f16)
        zb = sb("zb", [P, KT, COLS])
        zhb = sb("zhb", [P, KT, COLS])
        keepb = sb("keepb", [P, KT, COLS])
        tA = sb("tA", [P, RT, D])
        x1 = sb("x1", [P, RT, D])
        stA = sb("stA", [P, RT, 6])
        mvA = sb("mvA", [P, RT, 2])
        veA = sb("veA", [P, RT])
        rsA = sb("rsA", [P, RT])
        x2 = sb("x2", [P, RT, D])
        xf_hi = sb("xf_hi", [P, KT, COLS], f16)
        xf_lo = sb("xf_lo", [P, KT, COLS], f16)
        q_hi = sb("q_hi", [P, KT, COLS], f16)
        q_lo = sb("q_lo", [P, KT, COLS], f16)
        k_hi = sb("k_hi", [P, KT, COLS], f16)
        k_lo = sb("k_lo", [P, KT, COLS], f16)
        qs = sb("qs", [3 * HD, H, COLS], f16)
        ks = sb("ks", [3 * HD, H, COLS], f16)
        v_hi = sb("v_hi", [P, RT, H, HD + 2], f16)
        v_lo = sb("v_lo", [P, RT, H, HD], f16)
        sp = sb("sp", [P, 3, 2, N])
        s_min = sb("s_min", [P, 3, 2])
        p_sb = sb("p_sb", [P, 2, 2, N])
        pt_hi = sb("pt_hi", [P, 2, 2 * KT * P], f16)
        pt_lo = sb("pt_lo", [P, 2, 2 * KT * P], f16)
        rec = sb("rec", [P, 2, H])
        of_hi, of_lo = q_hi, q_lo
        stB = sb("stB", [P, RT, 6])
        mvB = sb("mvB", [P, RT, 2])
        veB = sb("veB", [P, RT])
        rsB = sb("rsB", [P, RT])

        psum = [ctx.enter_context(nc.psum_tensor(f"bank{i}", [P, COLS], f32)) for i in range(8)]
        X, Y = psum[0:2], psum[2:4]
        LOW, HIGH = psum[4:6], psum[6:8]
        SC, PT, OB = psum[4], psum[5:7], psum[7]

        S = {name: sem(name) for name in PER}
        w_in, w_set, w_hi_s, w_lo_s, id_s, one_s, half_s, masks_ready = (
            sem(n) for n in ("w_in", "w_set", "w_hi_done", "w_lo_done", "ident_ready", "ones_ready", "half_ready", "masks_ready"))
        passed = sem("passed")

        def has_before(g):
            return not isinstance(g, int) or g > 0

        def at(name, g, k):
            return g * PER[name] + k

        def settled(eng):
            eng.sem_inc(passed, 1)

        MI = {m: i for i, m in enumerate(MATS)}

        def w(m):
            i = MI[m]
            return W_hi[:, i], W_lo[:, i]

        HEAD, STEP_SLOTS = 12, 16
        A_SLOTS = HEAD + STEPS * STEP_SLOTS + 2
        UNIT0 = 12
        OUT0 = UNIT0 + UNITS + 3
        LAYER_SLOTS = OUT0 + 8
        B_SLOTS = 2 * LAYER_SLOTS + 5

        PACE = ((0, 0), (4, 1), (12, 9), (20, 14), (31, 22), (39, 29), (43, 30), (51, 38), (59, 42), (70, 50), (78, 56), (B_SLOTS, A_SLOTS))

        def step_of(k):
            if HEAD <= k < HEAD + STEPS * STEP_SLOTS:
                return divmod(k - HEAD, STEP_SLOTS)
            return None, None

        def layer_of(k):
            if k < 2 * LAYER_SLOTS:
                return divmod(k, LAYER_SLOTS)
            return None, None

        def unit(u):
            half, place = divmod(u, UNITS // 2)
            return place // 2, 2 * half + 4 * (place % 2), half, place % 4

        def next_group(g):
            return None if isinstance(g, int) and g == GROUPS - 1 else g + 1

        def mm3(o, l, r, start, stop, more=False):
            (lh, ll), (rh_, rl) = l, r
            nc.tensor.matmul(o, lh, rh_, start=start, stop=False, skip_group_check=more)
            nc.tensor.matmul(o, lh, rl, start=False, stop=False, skip_group_check=more)
            return nc.tensor.matmul(o, ll, rh_, start=False, stop=stop, skip_group_check=more)

        def by_feature(bank, m, act, t, start, stop, more=False):
            wh, wl = w(m)
            c = slice(t * P, t * P + P)
            for k in range(KT):
                last = mm3(bank[t][:, :], (wh[:, k, c], wl[:, k, c]),
                           (act[0][:, k, :], act[1][:, k, :]),
                           start and k == 0, stop and k == KT - 1, more)
            return last

        def by_node(bank, m, act, j):
            wh, wl = w(m)
            for i in range(2):
                c = slice((2 * j + i) * P, (2 * j + i + 1) * P)
                for k in range(KT):
                    last = mm3(bank[j][:, i * D:(i + 1) * D], (act[0][:, k, c], act[1][:, k, c]),
                               (wh[:, k, :], wl[:, k, :]), k == 0, k == KT - 1)
            return last

        def adj_product(t, hi, lo):
            ah, al = w("adjT")
            for b in range(GRAPHS):
                for k in range(KT):
                    r = b * KT + k
                    last = mm3(X[t][:, b * N:(b + 1) * N],
                               (hi[:, r, t * P:(t + 1) * P], lo[:, r, t * P:(t + 1) * P]),
                               (ah[:, k, :], al[:, k, :]), k == 0, k == KT - 1)
            return last

        def to_features(bank, src, t):
            for r in range(RT):
                last = nc.tensor.transpose(bank[t][:, r * P:(r + 1) * P], src[:, r, t * P:(t + 1) * P], ident[:, :])
            return last

        def to_nodes(bank, src, j):
            for i in range(2):
                r = 2 * j + i
                for t in range(KT):
                    last = nc.tensor.transpose(bank[j][:, i * D + t * P:i * D + (t + 1) * P],
                                               src[:, t, r * P:(r + 1) * P], ident[:, :])
            return last

        AF, HF, RH = (af_hi, af_lo), (hf_hi, hf_lo), (rh_hi, rh_lo)

        def pe_a(pe, g, k):
            later = has_before(g)
            s, c = step_of(k)
            if k in (0, 1):
                if k == 0:
                    pe.wait_ge(S["xn_lo"], at("xn_lo", g, 2))
                    if later:
                        pe.wait_ge(S["res_a"], at("res_a", g, 0))
                adj_product(k, xn_hi, xn_lo).then_inc(S["fill_x"], 1)
            if k in (4, 5):
                if k == 4:
                    pe.wait_ge(S["af_lo"], at("af_lo", g, 2))
                by_node(Y, "w0", AF, k - 4).then_inc(S["fill_y"], 1)
            if k == 9:
                pe.wait_ge(S["a_ln"], at("a_ln", g, 4))
                for t in range(KT):
                    to_features(X, x1, t).then_inc(S["fill_x"], 1)
            if s is None:
                return
            t = c % 2
            if c in (0, 1):
                if c == 0:
                    pe.wait_ge(S["hn_lo"], at("hn_lo", g, 2 + 2 * s))
                    if s == 0:
                        pe.wait_ge(S["hf_lo"], at("hf_lo", g, 2))
                        pe.wait_ge(S["hf32"], at("hf32", g, 2))
                adj_product(t, hn_hi, hn_lo).then_inc(S["fill_x"], 1)
            if c in (2, 3):
                if c == 2:
                    pe.wait_ge(S["hf_lo"], at("hf_lo", g, 2 + 2 * s))
                by_feature(Y, "u3", HF, t, True, False)
            if c in (4, 5):
                if c == 4:
                    pe.wait_ge(S["af_lo"], at("af_lo", g, 4 + 2 * s))
                by_feature(Y, "w4", AF, t, False, True).then_inc(S["fill_y"], 1)
            if c in (6, 7):
                pe.wait_ge(S["tr"], at("tr", g, 2 * s + t + 1))
                by_feature(Y, "w3", AF, t, False, True, more=True).then_inc(S["fill_y"], 1)
            if c in (8, 9):
                by_feature(X, "w5", AF, t, True, False)
            if c in (10, 11):
                if c == 10:
                    pe.wait_ge(S["rh_lo"], at("rh_lo", g, 2 * s + 2))
                by_feature(X, "u5", RH, t, False, True).then_inc(S["fill_x"], 1)
            if c == 14:
                pe.wait_ge(S["hf_new"], at("hf_new", g, 2 * s + 2))
                for j in range(2):
                    to_nodes(X, hF, j).then_inc(S["fill_x"], 1)

        def pe_b(pe, g, k):
            later = has_before(g)
            XF, OF = (xf_hi, xf_lo), (of_hi, of_lo)
            L, c = layer_of(k)
            if L is None:
                return
            wq_, wk_, wv_, wo_ = (("q2", "k2", "v2", "o2"), ("q3", "k3", "v3", "o3"))[L]
            u0 = UNITS * L
            if c == 0:
                if L == 0:
                    pe.wait_ge(S["a_ln"], at("a_ln", g, 8))
                else:
                    pe.wait_ge(S["b_ln"], at("b_ln", g, 4))
                for t in range(KT):
                    to_features(LOW, (x2, x3)[L], t).then_inc(S["xf_fill"], 1)
            if c in (3, 4):
                if c == 3:
                    pe.wait_ge(S["xf_lo"], at("xf_lo", g, 2 * L + 2))
                    if later or 2 * L > 0:
                        pe.wait_ge(S["res_b"], at("res_b", g, 2 * L))
                by_feature(HIGH, wq_, XF, c - 3, True, True).then_inc(S["qk_fill"], 1)
            if c in (5, 6):
                by_feature(LOW, wk_, XF, c - 5, True, True).then_inc(S["qk_fill"], 1)
            if c in (7, 8):
                if c == 7:
                    pe.wait_ge(S["q_lo"], at("q_lo", g, 2 * L + 2))
                by_node(HIGH, wv_, XF, c - 7).then_inc(S["v_fill"], 1)
            u = c - UNIT0
            if -1 <= u < UNITS - 1:
                if u < 0:
                    pe.wait_ge(S["k_lo"], at("k_lo", g, 2 * L + 2))
                    pe.wait_ge(S["stack1"], at("stack1", g, (L + 1) * 12 * 16))
                else:
                    pe.wait_ge(S["s_min"], at("s_min", g, 2 * (u0 + u + 1)))
                if u + 1 == UNITS // 2:
                    pe.wait_ge(S["stack2"], at("stack2", g, (L + 1) * 12 * 16))
                r, h0, half, place = unit(u + 1)
                b = r // KT
                for j in range(2):
                    h = h0 + j
                    last = nc.tensor.matmul(SC[:, j * N:(j + 1) * N],
                                            qs[:, h, r * P:(r + 1) * P], ks[:, h, b * N:(b + 1) * N],
                                            start=True, stop=True)
                last.then_inc(S["s_fill"], 1)
            if 0 <= u - 2 < UNITS:
                w_ = u - 2
                pe.wait_ge(S["pt_lo"], at("pt_lo", g, u0 + w_ + 1))
                r, h0, half, place = unit(w_)
                b = r // KT
                if place == 0 and w_ > 0:
                    pe.wait_ge(S["norm"], at("norm", g, RT * L + w_ // 4))
                for j in range(2):
                    h = h0 + j
                    o_ = OB[:, (2 * place + j) * (HD + 1):(2 * place + j + 1) * (HD + 1)]
                    for m in range(KT):
                        i = j * KT + m
                        ph = pt_hi[:, w_ % 2, i * P:(i + 1) * P]
                        pl = pt_lo[:, w_ % 2, i * P:(i + 1) * P]
                        vr = b * KT + m
                        nc.tensor.matmul(o_, ph, v_hi[:, vr, h, 0:HD + 1], start=m == 0, stop=False)
                        nc.tensor.matmul(o_[:, 0:HD], ph, v_lo[:, vr, h, :], start=False, stop=False)
                        last = nc.tensor.matmul(o_, pl, v_hi[:, vr, h, 0:HD + 1], start=False, stop=m == KT - 1)
                last.then_inc(S["pv"], 1)
            if 0 <= u < UNITS:
                pe.wait_ge(S["p_exp"], at("p_exp", g, 2 * (u0 + u + 1)))
                if u == 0:
                    pe.wait_ge(S["v_lo"], at("v_lo", g, 2 * L + 2))
                elif u > 1:
                    if later or u0 + u - 1 > 0:
                        pe.wait_ge(S["pt_lo"], at("pt_lo", g, u0 + u - 1))
                for j in range(2):
                    for m in range(KT):
                        i = j * KT + m
                        last = nc.tensor.transpose(PT[u % 2][:, i * P:(i + 1) * P],
                                                   p_sb[:, u % 2, j, m * P:(m + 1) * P], ident[:, :])
                last.then_inc(S["pt_fill"], 1)
            if c == OUT0:
                pe.wait_ge(S["norm"], at("norm", g, RT * (L + 1)))
                for t in range(KT):
                    to_features(LOW, oN, t).then_inc(S["of_fill"], 1)
            if c in (OUT0 + 3, OUT0 + 4):
                if c == OUT0 + 3:
                    pe.wait_ge(S["of_lo"], at("of_lo", g, 2 * L + 2))
                by_node(HIGH, wo_, OF, c - OUT0 - 3).then_inc(S["o_fill"], 1)

        def split_x_hi(act, g):
            later = has_before(g)
            if g is None:
                return
            act.wait_ge(S["x_loaded"], at("x_loaded", g, 16))
            if later or 2 - PER["fill_x"] > 0:
                act.wait_ge(S["fill_x"], at("fill_x", g, 2 - PER["fill_x"]))
            for j in range(2):
                nc.scalar.activation(xn_hi[:, 2 * j:2 * j + 2, :], xin[:, 2 * j:2 * j + 2, :], ACT.Copy).then_inc(S["xn_hi"], 1)

        def act_a(act, g, k):
            later = has_before(g)
            A = nc.scalar.activation
            s, c = step_of(k)
            if k in (1, 2):
                act.wait_ge(S["fill_x"], at("fill_x", g, k))
                A(af_hi[:, k - 1, :], X[k - 1][:, :], ACT.Copy).then_inc(S["af_hi"], 1)
            if k == 9:
                act.wait_ge(S["a_ln"], at("a_ln", g, 4))
                for j in range(2):
                    A(hn_hi[:, 2 * j:2 * j + 2, :], x1[:, 2 * j:2 * j + 2, :], ACT.Copy).then_inc(S["hn_hi"], 1)
            if k == 10:
                for t in range(KT):
                    act.wait_ge(S["fill_x"], at("fill_x", g, 2 + t + 1))
                    A(hf_hi[:, t, :], X[t][:, :], ACT.Copy).then_inc(S["hf_hi"], 1)
                    A(hF[:, t, :], X[t][:, :], ACT.Copy).then_inc(S["hf32"], 1)
            if s is None:
                return
            fx = 4 + 6 * s
            fy = 2 + 4 * s
            if c in (1, 2):
                t = c - 1
                act.wait_ge(S["fill_x"], at("fill_x", g, fx + t + 1))
                A(af_hi[:, t, :], X[t][:, :], ACT.Copy).then_inc(S["af_hi"], 1)
            if s == 1 and c == 4:
                split_x_hi(act, next_group(g))
            if c in (5, 6):
                t = c - 5
                act.wait_ge(S["fill_y"], at("fill_y", g, fy + t + 1))
                A(trb[:, t, :], Y[t][:, :], ACT.Tanh, bias=bias[:, 1, t:t + 1], scale=0.5 / WS).then_inc(S["tr"], 1)
            if c in (7, 8):
                t = c - 7
                act.wait_ge(S["rh"], at("rh", g, 2 * s + t + 1))
                A(rh_hi[:, t, :], rhb[:, t, :], ACT.Copy).then_inc(S["rh_hi"], 1)
                act.wait_ge(S["fill_y"], at("fill_y", g, fy + 2 + t + 1))
                A(tzb[:, t, :], Y[t][:, :], ACT.Tanh, bias=bias[:, 0, t:t + 1], scale=0.5 / WS).then_inc(S["tz"], 1)
            if c in (11, 12):
                t = c - 11
                act.wait_ge(S["fill_x"], at("fill_x", g, fx + 2 + t + 1))
                A(tvb[:, t, :], X[t][:, :], ACT.Tanh, bias=bias[:, 2, t:t + 1], scale=1.0 / WS).then_inc(S["tv"], 1)
            if c in (13, 14) and s < STEPS - 1:
                t = c - 13
                act.wait_ge(S["hf_new"], at("hf_new", g, 2 * s + t + 1))
                A(hf_hi[:, t, :], hF[:, t, :], ACT.Copy).then_inc(S["hf_hi"], 1)
            if c == 15 and s < STEPS - 1:
                for j in range(2):
                    act.wait_ge(S["fill_x"], at("fill_x", g, fx + 4 + j + 1))
                    A(hn_hi[:, 2 * j:2 * j + 2, :], X[j][:, :].rearrange("p (a b) -> p a b", a=2), ACT.Copy).then_inc(S["hn_hi"], 1)

        def act_b(act, g, k):
            later = has_before(g)
            A = nc.scalar.activation
            L, c = layer_of(k)
            if L is None:
                return
            u0 = UNITS * L
            if c == 1:
                for t in range(KT):
                    act.wait_ge(S["xf_fill"], at("xf_fill", g, 2 * L + t + 1))
                    A(xf_hi[:, t, :], LOW[t][:, :], ACT.Copy).then_inc(S["xf_hi"], 1)
            if c in (4, 5, 6, 7):
                m, t = divmod(c - 4, 2)
                name, buf, bank = (("q_hi", q_hi, HIGH), ("k_hi", k_hi, LOW))[m]
                act.wait_ge(S["qk_fill"], at("qk_fill", g, 4 * L + 2 * m + t + 1))
                if L == 0:
                    A(buf[:, t, :], bank[t][:, :], ACT.Identity, bias=bias[:, 3 + m, t:t + 1], scale=1.0).then_inc(S[name], 1)
                else:
                    A(buf[:, t, :], bank[t][:, :], ACT.Copy).then_inc(S[name], 1)
            if c in (8, 9):
                j = c - 8
                act.wait_ge(S["v_fill"], at("v_fill", g, 2 * L + j + 1))
                A(v_hi[:, 2 * j:2 * j + 2, :, 0:HD].rearrange("p a h d -> p (a h) d"),
                  HIGH[j][:, :].rearrange("p (h d) -> p h d", d=HD), ACT.Copy, scale=1.0 / WS).then_inc(S["v_hi"], 1)
            u = c - UNIT0
            if 0 <= u - 1 < UNITS:
                act.wait_ge(S["pt_fill"], at("pt_fill", g, u0 + u))
                if later or u0 + u - 2 > 0:
                    act.wait_ge(S["pv"], at("pv", g, u0 + u - 2))
                A(pt_hi[:, (u - 1) % 2, :], PT[(u - 1) % 2][:, :], ACT.Copy).then_inc(S["pt_hi"], 1)
            if -1 <= u < UNITS - 1:
                n = u + 1
                if later or u0 + n - 1 > 0:
                    act.wait_ge(S["pt_fill"], at("pt_fill", g, u0 + n - 1))
                for j in range(2):
                    act.wait_ge(S["s_min"], at("s_min", g, 2 * (u0 + n) + j + 1))
                    A(p_sb[:, n % 2, j, :], sp[:, n % 3, j, :], ACT.Exp, bias=s_min[:, n % 3, j:j + 1], scale=-1.0).then_inc(S["p_exp"], 1)
            if c == OUT0 + 1:
                for t in range(KT):
                    act.wait_ge(S["of_fill"], at("of_fill", g, 2 * L + t + 1))
                    if L == 0:
                        A(of_hi[:, t, :], LOW[t][:, :], ACT.Identity, bias=bias_in[:, 7, t:t + 1], scale=1.0).then_inc(S["of_hi"], 1)
                    else:
                        A(of_hi[:, t, :], LOW[t][:, :], ACT.Copy).then_inc(S["of_hi"], 1)

        V = nc.vector

        def stats(dve, src, st, mv, names, g, n):
            later = has_before(g)
            s_st, s_mv, s_ve = names
            if later or RT * n > 0:
                dve.wait_ge(S[s_mv], at(s_mv, g, RT * n))
            for r in range(RT):
                V.bn_stats(st[:, r, :], src[:, r, :]).then_inc(S[s_st], 1)
            dve.wait_ge(S[s_st], at(s_st, g, RT * (n + 1)))
            settled(dve)
            for r in range(RT):
                V.bn_aggr(mv[:, r, :], st[:, r, :]).then_inc(S[s_mv], 1)

        def normalise(dve, dst, src, mv, rs, names, g, n):
            later = has_before(g)
            s_rs, s_ln = names
            dve.wait_ge(S[s_rs], at(s_rs, g, n + 1))
            for r in range(RT):
                V.tensor_scalar(dst[:, r, :], src[:, r, :], mv[:, r, 0:1], rs[:, r:r + 1],
                                ALU.subtract, ALU.mult).then_inc(S[s_ln], 1)

        def low_part(dve, name, lo, src, hi):
            V.tensor_tensor(lo, src, hi, ALU.subtract).then_inc(S[name], 1)

        def split_x_lo(dve, g):
            later = has_before(g)
            if g is None:
                return
            dve.wait_ge(S["x_loaded"], at("x_loaded", g, 16))
            for j in range(2):
                dve.wait_ge(S["xn_hi"], at("xn_hi", g, j + 1))
                low_part(dve, "xn_lo", xn_lo[:, 2 * j:2 * j + 2, :], xin[:, 2 * j:2 * j + 2, :], xn_hi[:, 2 * j:2 * j + 2, :])

        def dve_a(dve, g, k):
            later = has_before(g)
            s, c = step_of(k)
            if k in (2, 3):
                dve.wait_ge(S["af_hi"], at("af_hi", g, k - 1))
                low_part(dve, "af_lo", af_lo[:, k - 2, :], X[k - 2][:, :], af_hi[:, k - 2, :])
            if k in (5, 6):
                j = k - 5
                dve.wait_ge(S["xb"], at("xb", g, 1))
                dve.wait_ge(S["fill_y"], at("fill_y", g, j + 1))
                V.scalar_tensor_tensor(out=tA[:, 2 * j:2 * j + 2, :].rearrange("p a b -> p (a b)"), in0=Y[j][:, :], scalar=1.0 / WS,
                                       in1=xb[:, 2 * j:2 * j + 2, :].rearrange("p a b -> p (a b)"),
                                       op0=ALU.mult, op1=ALU.add).then_inc(S["res_a"], 1)
                if j == 1:
                    dve.wait_ge(S["res_a"], at("res_a", g, 2))
                    stats(dve, tA, stA, mvA, ("a_st", "a_mv", "a_ve"), g, 0)
            if k == 8:
                normalise(dve, x1, tA, mvA, rsA, ("a_rs", "a_ln"), g, 0)
            if k == 11:
                for t in range(KT):
                    dve.wait_ge(S["hf32"], at("hf32", g, t + 1))
                    low_part(dve, "hf_lo", hf_lo[:, t, :], X[t][:, :], hf_hi[:, t, :])
            if k == A_SLOTS - 1:
                if later:
                    dve.wait_ge(S["xb2"], at("xb2", g, 0))
                if later:
                    dve.wait_ge(S["xf_fill"], at("xf_fill", g, -2))
                normalise(dve, x2, tA, mvA, rsA, ("a_rs", "a_ln"), g, 1)
            if s is None:
                return
            fx = 4 + 6 * s
            t = c % 2
            if c in (2, 3):
                dve.wait_ge(S["af_hi"], at("af_hi", g, 2 + 2 * s + t + 1))
                low_part(dve, "af_lo", af_lo[:, t, :], X[t][:, :], af_hi[:, t, :])
            if s == 1 and c == 5:
                split_x_lo(dve, next_group(g))
            if c in (6, 7):
                dve.wait_ge(S["tr"], at("tr", g, 2 * s + t + 1))
                V.scalar_tensor_tensor(out=rhb[:, t, :], in0=trb[:, t, :], scalar=1.0, in1=hF[:, t, :],
                                       op0=ALU.add, op1=ALU.mult).then_inc(S["rh"], 1)
            if c in (8, 9):
                dve.wait_ge(S["rh_hi"], at("rh_hi", g, 2 * s + t + 1))
                low_part(dve, "rh_lo", rh_lo[:, t, :], rhb[:, t, :], rh_hi[:, t, :])
                dve.wait_ge(S["tz"], at("tz", g, 2 * s + t + 1))
                V.tensor_scalar(zb[:, t, :], tzb[:, t, :], 0.5, 0.5, ALU.mult, ALU.add).then_inc(S["z"], 1)
            if c in (12, 13):
                dve.wait_ge(S["tv"], at("tv", g, 2 * s + t + 1))
                V.tensor_tensor(tvb[:, t, :], tvb[:, t, :], zb[:, t, :], ALU.mult).then_inc(S["zv"], 1)
                dve.wait_ge(S["zv"], at("zv", g, 2 * s + t + 1))
                dve.wait_ge(S["keep"], at("keep", g, 2 * s + t + 1))
                V.tensor_tensor(hF[:, t, :], tvb[:, t, :], keepb[:, t, :], ALU.add).then_inc(S["hf_new"], 1)
            if c == 15 and s < STEPS - 1:
                for j in range(2):
                    dve.wait_ge(S["hn_hi"], at("hn_hi", g, 2 + 2 * s + j + 1))
                    low_part(dve, "hn_lo", hn_lo[:, 2 * j:2 * j + 2, :].rearrange("p a b -> p (a b)"), X[j][:, :],
                             hn_hi[:, 2 * j:2 * j + 2, :].rearrange("p a b -> p (a b)"))
            if c == 15 and s == STEPS - 1:
                for j in range(2):
                    dve.wait_ge(S["fill_x"], at("fill_x", g, fx + 4 + j + 1))
                    V.tensor_tensor(tA[:, 2 * j:2 * j + 2, :].rearrange("p a b -> p (a b)"), X[j][:, :],
                                    x1[:, 2 * j:2 * j + 2, :].rearrange("p a b -> p (a b)"), ALU.add).then_inc(S["res_a"], 1)
                dve.wait_ge(S["res_a"], at("res_a", g, 4))
                stats(dve, tA, stA, mvA, ("a_st", "a_mv", "a_ve"), g, 1)

        def dve_b(dve, g, k):
            later = has_before(g)
            L, c = layer_of(k)
            names = ("b_st", "b_mv", "b_ve")
            if k == 2 * LAYER_SLOTS + 1:
                dve.wait_ge(S["gam"], at("gam", g, 1))
                V.tensor_tensor(tF[:, :, :], o_g[:, :, :], obe[:, :, :], ALU.add).then_inc(S["t_fin"], 1)
                dve.wait_ge(S["t_fin"], at("t_fin", g, 1))
                stats(dve, tF, stB, mvB, names, g, 2)
            if k == 2 * LAYER_SLOTS + 3:
                if later:
                    dve.wait_ge(S["stored"], at("stored", g, 0))
                normalise(dve, y_out, tF, mvB, rsB, ("b_rs", "b_ln"), g, 2)
            if L is None:
                return
            u0 = UNITS * L
            if c == 2:
                for t in range(KT):
                    dve.wait_ge(S["xf_hi"], at("xf_hi", g, 2 * L + t + 1))
                    low_part(dve, "xf_lo", xf_lo[:, t, :], LOW[t][:, :], xf_hi[:, t, :])
            if c in (5, 6, 7, 8):
                m, t = divmod(c - 5, 2)
                his, los, hi, lo, bank = (("q_hi", "q_lo", q_hi, q_lo, HIGH), ("k_hi", "k_lo", k_hi, k_lo, LOW))[m]
                dve.wait_ge(S[his], at(his, g, 2 * L + t + 1))
                if L == 0:
                    V.scalar_tensor_tensor(out=lo[:, t, :], in0=bank[t][:, :], scalar=bias[:, 3 + m, t:t + 1],
                                           in1=hi[:, t, :], op0=ALU.add, op1=ALU.subtract).then_inc(S[los], 1)
                else:
                    low_part(dve, los, lo[:, t, :], bank[t][:, :], hi[:, t, :])
            if c in (9, 10):
                j = c - 9
                dve.wait_ge(S["v_hi"], at("v_hi", g, 2 * L + j + 1))
                V.scalar_tensor_tensor(out=v_lo[:, 2 * j:2 * j + 2, :, :].rearrange("p a h d -> p (a h) d"),
                                       in0=HIGH[j][:, :].rearrange("p (h d) -> p h d", d=HD), scalar=1.0 / WS,
                                       in1=v_hi[:, 2 * j:2 * j + 2, :, 0:HD].rearrange("p a h d -> p (a h) d"),
                                       op0=ALU.mult, op1=ALU.subtract).then_inc(S["v_lo"], 1)
            u = c - UNIT0
            if -1 <= u < UNITS - 1:
                n = u + 1
                dve.wait_ge(S["s_fill"], at("s_fill", g, u0 + n + 1))
                if later or 2 * (u0 + n) - 4 > 0:
                    dve.wait_ge(S["p_exp"], at("p_exp", g, 2 * (u0 + n) - 4))
                settled(dve)
                for j in range(2):
                    V.tensor_tensor_reduce(out=sp[:, n % 3, j, :], in0=SC[:, j * N:(j + 1) * N],
                                           in1=neg_mask[:, L, unit(n)[0] % KT, :], scale=1.0 / (WS * WS), scalar=3.0e38,
                                           op0=ALU.add, op1=ALU.min,
                                           accum_out=s_min[:, n % 3, j:j + 1]).then_inc(S["s_min"], 1)
            if 0 <= u - 1 < UNITS:
                dve.wait_ge(S["pt_hi"], at("pt_hi", g, u0 + u))
                low_part(dve, "pt_lo", pt_lo[:, (u - 1) % 2, :], PT[(u - 1) % 2][:, :], pt_hi[:, (u - 1) % 2, :])
            if u >= 2 and (u - 2) % 4 == 3 and u - 2 < UNITS:
                n = (u - 2) // 4
                r, h0, half, place = unit(u - 2)
                o_ = OB[:, 0:H * (HD + 1)].rearrange("p (h d) -> p h d", d=HD + 1)
                if later or u0 + u - 1 > 0:
                    dve.wait_ge(S["pv"], at("pv", g, u0 + u - 1))
                V.reciprocal(rec[:, n % 2, :], o_[:, :, HD]).then_inc(S["rec"], 1)
                dve.wait_ge(S["rec"], at("rec", g, RT * L + n + 1))
                V.tensor_tensor(oN[:, r - 1:r + 1, :].rearrange("p r (a f j d) -> p (r a) f j d", a=2, f=2, j=2)[:, :, half],
                                OB[:, 0:H * (HD + 1)].rearrange("p (w j d) -> p w j d", w=4, j=2)[:, :, :, 0:HD],
                                rec[:, n % 2, :].rearrange("p (w j) -> p w j", j=2).unsqueeze(3).to_broadcast([P, 4, 2, HD]),
                                ALU.mult).then_inc(S["norm"], 1)
            if c == OUT0 + 2:
                for t in range(KT):
                    dve.wait_ge(S["of_hi"], at("of_hi", g, 2 * L + t + 1))
                    if L == 0:
                        V.scalar_tensor_tensor(out=of_lo[:, t, :], in0=LOW[t][:, :], scalar=bias_in[:, 7, t:t + 1],
                                               in1=of_hi[:, t, :], op0=ALU.add, op1=ALU.subtract).then_inc(S["of_lo"], 1)
                    else:
                        low_part(dve, "of_lo", of_lo[:, t, :], LOW[t][:, :], of_hi[:, t, :])
            if c in (OUT0 + 4, OUT0 + 5):
                j = c - OUT0 - 4
                dve.wait_ge(S["o_fill"], at("o_fill", g, 2 * L + j + 1))
                if L == 0:
                    dve.wait_ge(S["xb2"], at("xb2", g, 1))
                    if later:
                        dve.wait_ge(S["obe"], at("obe", g, 0))
                    V.scalar_tensor_tensor(out=tB[:, 2 * j:2 * j + 2, :].rearrange("p a b -> p (a b)"), in0=HIGH[j][:, :],
                                           scalar=1.0 / WS, in1=xb2[:, 2 * j:2 * j + 2, :].rearrange("p a b -> p (a b)"),
                                           op0=ALU.mult, op1=ALU.add).then_inc(S["res_b"], 1)
                else:
                    V.scalar_tensor_tensor(out=tB[:, 2 * j:2 * j + 2, :], in0=HIGH[j][:, :].rearrange("p (a b) -> p a b", a=2),
                                           scalar=1.0 / WS, in1=bp_r.unsqueeze(1).to_broadcast([P, 2, D]),
                                           op0=ALU.mult, op1=ALU.add).then_inc(S["res_b"], 1)
                if j == 1:
                    dve.wait_ge(S["res_b"], at("res_b", g, 2 * L + 2))
                    stats(dve, tB, stB, mvB, names, g, L)
            if c == LAYER_SLOTS - 1:
                if L == 0:
                    normalise(dve, x3, tB, mvB, rsB, ("b_rs", "b_ln"), g, 0)
                else:
                    normalise(dve, o_n, tB, mvB, rsB, ("b_rs", "b_ln"), g, 1)

        G = nc.gpsimd

        def rstd(pool, mv, ve, rs, names, g, n):
            later = has_before(g)
            s_mv, s_ve, s_rs = names
            pool.wait_ge(S[s_mv], at(s_mv, g, RT * (n + 1)))
            if later or n > 0:
                pool.wait_ge(S[s_rs], at(s_rs, g, n))
            G.tensor_tensor(ve[:, :], mv[:, :, 1], eps_t[:, :], ALU.add).then_inc(S[s_ve], 1)
            pool.wait_ge(S[s_ve], at(s_ve, g, n + 1))
            G.tensor_tensor(rs[:, :], ve[:, :], m_half[:, :], ALU.pow).then_inc(S[s_rs], 1)

        def add_bias(pool, g):
            later = has_before(g)
            if g is None:
                return
            pool.wait_ge(S["x_loaded"], at("x_loaded", g, 16))
            if later:
                pool.wait_ge(S["res_a"], at("res_a", g, -2))
            G.tensor_tensor(xb[:, :, :], xin[:, :, :], b0_r.unsqueeze(1).to_broadcast([P, RT, D]), ALU.add).then_inc(S["xb"], 1)

        def pool_a(pool, g, k):
            later = has_before(g)
            s, c = step_of(k)
            names = ("a_mv", "a_ve", "a_rs")
            if k == 7:
                rstd(pool, mvA, veA, rsA, names, g, 0)
            if k == 10:
                for j in range(2):
                    pool.wait_ge(S["hn_hi"], at("hn_hi", g, j + 1))
                    G.tensor_tensor(hn_lo[:, 2 * j:2 * j + 2, :], x1[:, 2 * j:2 * j + 2, :], hn_hi[:, 2 * j:2 * j + 2, :],
                                    ALU.subtract).then_inc(S["hn_lo"], 1)
            if k == A_SLOTS - 2:
                rstd(pool, mvA, veA, rsA, names, g, 1)
            if s is None:
                return
            if s == 1 and c == 5:
                add_bias(pool, next_group(g))
            if c in (9, 10):
                t = c - 9
                pool.wait_ge(S["z"], at("z", g, 2 * s + t + 1))
                G.tensor_tensor(zhb[:, t, :], zb[:, t, :], hF[:, t, :], ALU.mult).then_inc(S["zh"], 1)
                pool.wait_ge(S["zh"], at("zh", g, 2 * s + t + 1))
                G.tensor_tensor(keepb[:, t, :], hF[:, t, :], zhb[:, t, :], ALU.subtract).then_inc(S["keep"], 1)
            if c in (14, 15) and s < STEPS - 1:
                t = c - 14
                pool.wait_ge(S["hf_hi"], at("hf_hi", g, 2 + 2 * s + t + 1))
                G.tensor_tensor(hf_lo[:, t, :], hF[:, t, :], hf_hi[:, t, :], ALU.subtract).then_inc(S["hf_lo"], 1)

        def pool_b(pool, g, k):
            later = has_before(g)
            names = ("b_mv", "b_ve", "b_rs")
            if k == 0:
                pool.wait_ge(S["a_ln"], at("a_ln", g, 8))
                G.tensor_tensor(xb2[:, :, :], x2[:, :, :], bo_r.unsqueeze(1).to_broadcast([P, RT, D]), ALU.add).then_inc(S["xb2"], 1)
            if k == LAYER_SLOTS - 2:
                rstd(pool, mvB, veB, rsB, names, g, 0)
            if k == LAYER_SLOTS + 1:
                pool.wait_ge(S["b_ln"], at("b_ln", g, 4))
                G.tensor_tensor(xbe[:, :, :], x3[:, :, :], bet_r.unsqueeze(1).to_broadcast([P, RT, D]), ALU.add).then_inc(S["xbe"], 1)
            if k == 2 * LAYER_SLOTS - 2:
                rstd(pool, mvB, veB, rsB, names, g, 1)
                pool.wait_ge(S["res_b"], at("res_b", g, 4))
                pool.wait_ge(S["xbe"], at("xbe", g, 1))
                G.tensor_tensor(obe[:, :, :], xbe[:, :, :], tB[:, :, :], ALU.add).then_inc(S["obe"], 1)
            if k == 2 * LAYER_SLOTS:
                pool.wait_ge(S["b_ln"], at("b_ln", g, 8))
                G.tensor_tensor(o_g[:, :, :], o_n[:, :, :], gam_r.unsqueeze(1).to_broadcast([P, RT, D]), ALU.mult).then_inc(S["gam"], 1)
            if k == 2 * LAYER_SLOTS + 2:
                rstd(pool, mvB, veB, rsB, names, g, 2)

        def load_x(sp_, g):
            later = has_before(g)
            if later:
                sp_.wait_ge(S["xn_hi"], at("xn_hi", g, 0))
            if later:
                sp_.wait_ge(S["xn_lo"], at("xn_lo", g, 0))
            if later:
                sp_.wait_ge(S["xb"], at("xb", g, 0))
            settled(sp_)
            sp_.dma_start(xin[:, :, :], x_v[g]).then_inc(S["x_loaded"], 16)

        def sp_a(sp_, g, k):
            later = has_before(g)
            if k == 8 and next_group(g) is not None:
                load_x(sp_, next_group(g))

        def sp_b(sp_, g, k):
            later = has_before(g)
            L, c = layer_of(k)
            if k == 2 * LAYER_SLOTS + 4:
                sp_.wait_ge(S["b_ln"], at("b_ln", g, 12))
                settled(sp_)
                sp_.dma_start(out_v[g], y_out[:, :, :]).then_inc(S["stored"], 16)
            if L is not None and c in (7, 9):
                Q = (qs, (q_hi, q_hi, q_lo))
                K = (ks, (k_hi, k_lo, k_hi))
                low = "q_lo" if c == 7 else "k_lo"
                sp_.wait_ge(S[low], at(low, g, 2 * L + 2))
                for (dst, parts), half in (((Q, 0),) if c == 7 else ((K, 0), (Q, 1), (K, 1))):
                    for i in (2 * half, 2 * half + 1):
                        for m, src in enumerate(parts):
                            sp_.dma_start(dst[m * HD:(m + 1) * HD, i:H:P // HD, :],
                                          src[i * HD:(i + 1) * HD, :, :]).then_inc(S[("stack1", "stack2")[half]], 16)

        def merged(eng, a, ga, b, gb):
            done = 0
            for (b0_, a0_), (b1_, a1_) in zip(PACE, PACE[1:]):
                for i in range(b0_, b1_):
                    b(eng, gb, i)
                    while (done - a0_) * (b1_ - b0_) < (i + 1 - b0_) * (a1_ - a0_):
                        a(eng, ga, done)
                        done += 1

        def whole(eng, a, b):
            for k in range(A_SLOTS):
                a(eng, 0, k)
            merged(eng, a, 1, b, 0)
            with eng.Fori(2, GROUPS - 1) as g:
                merged(eng, a, g, b, g - 1)
            merged(eng, a, GROUPS - 1, b, GROUPS - 2)
            for k in range(B_SLOTS):
                b(eng, GROUPS - 1, k)

        block = ctx.enter_context(nc.Block())

        @block.sync
        def _(sp_):
            load_x(sp_, 0)
            plain = [adjT, w0, w3T[0:D, :], w4T[0:D, :], w5T[0:D, :], u3T, u5T, wq, wk, wv, wo,
                     wqkv[:, 0:D], wqkv[:, D:2 * D], wqkv[:, 2 * D:3 * D], wproj]
            n = 0
            for i, m in enumerate(plain):
                sp_.dma_start(raw[:, i], rows(m)).then_inc(w_in, 16)
                n += 1
            for i, m in enumerate((w3T, w4T, w5T)):
                sp_.dma_start(raw2[:, i], rows(m[D:2 * D, :])).then_inc(w_in, 16)
                n += 1
            sp_.dma_start(adj_sb[:, :, :], rows(adj)).then_inc(w_in, 16)
            for i, v in enumerate((b0, bo, bproj, gamma, beta)):
                sp_.dma_start(rep[:, i, :], v.rearrange("(a n) -> a n", a=1).to_broadcast([P, D])).then_inc(w_in, 16)
            for i, v in enumerate((b3, b4, b5, bu3, bu5, bq, bk, bv)):
                sp_.dma_start(bias_in[:, i, :], v.rearrange("(t p) -> p t", p=P), allow_slow_non_contiguous=True).then_inc(w_in, 16)
            whole(sp_, sp_a, sp_b)
            sp_.wait_ge(S["stored"], GROUPS * 16)

        N_IN = 15 + 3 + 1 + 5 + 8

        @block.tensor
        def _(pe):
            pe.wait_ge(id_s, 2)
            pe.wait_ge(w_lo_s, len(MATS))
            pe.wait_ge(one_s, 1)
            whole(pe, pe_a, pe_b)

        @block.scalar
        def _(act):
            act.wait_ge(w_in, N_IN * 16)
            for i, m in enumerate(MATS):
                if m in ("w3", "w4", "w5"):
                    act.wait_ge(w_set, 4)
                nc.scalar.activation(W_hi[:, i], raw[:, i], ACT.Copy, scale=SCALE[m]).then_inc(w_hi_s, 1)
            act.wait_ge(masks_ready, 9)
            split_x_hi(act, 0)
            whole(act, act_a, act_b)

        @block.vector
        def _(dve):
            V.memset(v_hi[:, :, :, :], 1.0).then_inc(one_s, 1)
            dve.wait_ge(w_in, N_IN * 16)
            for i in range(3):
                V.tensor_tensor(raw[:, 2 + i], raw[:, 2 + i], raw2[:, i], ALU.add).then_inc(w_set, 1)
            dve.wait_ge(w_set, 3)
            V.tensor_tensor(raw[:, 2], raw[:, 2], raw[:, 3], ALU.subtract).then_inc(w_set, 1)
            dve.wait_ge(w_set, 4)
            for i, m in enumerate(MATS):
                dve.wait_ge(w_hi_s, i + 1)
                V.scalar_tensor_tensor(out=W_lo[:, i], in0=raw[:, i], scalar=SCALE[m], in1=W_hi[:, i],
                                       op0=ALU.mult, op1=ALU.subtract).then_inc(w_lo_s, 1)
            V.tensor_scalar(neg_mask[:, 0], adj_sb[:, :, :], -1.0, 1.0, ALU.mult, ALU.add).then_inc(masks_ready, 1)
            V.tensor_scalar(neg_mask[:, 1], adj_sb[:, :, :], 0.0, MASK_L3, ALU.is_equal, ALU.mult).then_inc(masks_ready, 1)
            V.tensor_tensor(bias[:, 0, :], bias_in[:, 0, :], bias_in[:, 3, :], ALU.add).then_inc(masks_ready, 1)
            V.tensor_tensor(bias[:, 1, :], bias_in[:, 1, :], bias_in[:, 3, :], ALU.add).then_inc(masks_ready, 1)
            V.tensor_tensor(bias[:, 2, :], bias_in[:, 2, :], bias_in[:, 4, :], ALU.add).then_inc(masks_ready, 1)
            V.tensor_scalar(bias[:, 3, :], bias_in[:, 5, :], -WS * QK, None, ALU.mult).then_inc(masks_ready, 1)
            V.tensor_scalar(bias[:, 4, :], bias_in[:, 6, :], WS, None, ALU.mult).then_inc(masks_ready, 1)
            dve.wait_ge(masks_ready, 7)
            V.tensor_scalar(neg_mask[:, 0], neg_mask[:, 0], MASK_L2 * WS * WS, None, ALU.mult).then_inc(masks_ready, 1)
            V.tensor_scalar(bias[:, 0:2, :], bias[:, 0:2, :], 0.5, None, ALU.mult).then_inc(masks_ready, 1)
            dve.wait_ge(masks_ready, 9)
            dve.wait_ge(one_s, 1)
            split_x_lo(dve, 0)
            whole(dve, dve_a, dve_b)

        @block.gpsimd
        def _(pool):
            G.memset(ident[:, :], 0.0).then_inc(id_s, 1)
            G.memset(m_half[:, :], -0.5).then_inc(half_s, 1)
            G.memset(eps_t[:, :], EPS).then_inc(half_s, 1)
            pool.wait_ge(id_s, 1)
            G.affine_select(out=ident[:, :], in_=ident[:, :], compare_op=ALU.not_equal, fill=1.0, base=0,
                            pattern=[[-1, P]], channel_multiplier=1).then_inc(id_s, 1)
            pool.wait_ge(half_s, 2)
            pool.wait_ge(w_in, N_IN * 16)
            add_bias(pool, 0)
            whole(pool, pool_a, pool_b)


def kernel(**inputs):
    import numpy as np
    import concourse.bacc as bacc
    from concourse import mybir as _mybir
    from concourse.bass_utils import run_bass_kernel_spmd

    def a(name):
        return np.ascontiguousarray(inputs[name])

    def t(name):
        return np.ascontiguousarray(np.asarray(inputs[name]).T)

    arrays = dict(
        x=a("x").reshape(B * N, D), adj=a("adj"), adjT=t("adj"), w0=a("L0_gnn_weight"), b0=a("L0_gnn_bias"),
        w3T=t("L1_gnn_w3_w"), b3=a("L1_gnn_w3_b"), u3T=t("L1_gnn_u3_w"), bu3=a("L1_gnn_u3_b"),
        w4T=t("L1_gnn_w4_w"), b4=a("L1_gnn_w4_b"), w5T=t("L1_gnn_w5_w"), b5=a("L1_gnn_w5_b"),
        u5T=t("L1_gnn_u5_w"), bu5=a("L1_gnn_u5_b"),
        wq=a("L2_gnn_Wq"), bq=a("L2_gnn_bq"), wk=a("L2_gnn_Wk"), bk=a("L2_gnn_bk"),
        wv=a("L2_gnn_Wv"), bv=a("L2_gnn_bv"), wo=a("L2_gnn_Wo"), bo=a("L2_gnn_bo"),
        wqkv=a("L3_gnn_w_qkv"), wproj=a("L3_gnn_w_proj"), bproj=a("L3_gnn_b_proj"),
        gamma=a("L3_gnn_ln_gamma"), beta=a("L3_gnn_ln_beta"))
    nc = bacc.Bacc("TRN2", target_bir_lowering=False, num_devices=1)
    args = [nc.dram_tensor(f"in_{n}", v.shape, _mybir.dt.from_np(v.dtype), kind="ExternalInput").ap() for n, v in arrays.items()]
    args.append(nc.dram_tensor("out", (B * N, D), _mybir.dt.float32, kind="ExternalOutput").ap())
    gnn_stack_kernel(nc, *args)
    r = run_bass_kernel_spmd(nc, [{f"in_{n}": v for n, v in arrays.items()}], core_ids=[0])
    return r.results[0]["out"].reshape(B, N, D)
```

```python
import concourse.bass as bass
from concourse import mybir
from contextlib import ExitStack
import math

B, N, D, H = 32, 256, 256, 8
HD = D // H
P = 128
GRAPHS = 2
COLS = GRAPHS * N
GROUPS = B // GRAPHS
RT = COLS // P
KT = D // P
STEPS = 3
UNITS = RT * H // 2
EPS = 1e-5
WS = 64.0
QK = 1.0 / math.sqrt(HD)
MASK_L2 = 1e9
MASK_L3 = 3.0e38

PER = dict(
    x_loaded=16, xb=1, xn_hi=2, xn_lo=2, hn_hi=6, hn_lo=6, fill_x=16, fill_y=20, af_hi=8, af_lo=8, res_a=4,
    hf32=2, hf_hi=6, hf_lo=6, tr=6, tz=6, tv=6, rh=6, rh_hi=6, rh_lo=6, zh=6, keep=6, zv=6, hf_new=6,
    a_st=8, a_mv=8, a_ve=3, a_rs=2, a_ln=8,
    xb2=1, xf_fill=4, xf_hi=4, xf_lo=4, qk_fill=8, q_hi=4, q_lo=4, k_hi=4, k_lo=4,
    v_fill=4, v_hi=4, v_lo=4, stack1=2 * 12 * 16, stack2=2 * 12 * 16, s_fill=2 * UNITS, s_min=4 * UNITS, p_exp=4 * UNITS, pt_fill=2 * UNITS,
    pt_hi=2 * UNITS, pt_lo=2 * UNITS, pv=2 * UNITS, rec=8, norm=8, of_fill=4, of_hi=4, of_lo=4, o_fill=4, res_b=4,
    gam=1, xbe=1, obe=1, t_fin=1,
    b_st=12, b_mv=12, b_ve=3, b_rs=3, b_ln=12, stored=16,
)

MATS = ["adjT", "w0", "w3", "w4", "w5", "u3", "u5", "q2", "k2", "v2", "o2", "q3", "k3", "v3", "o3"]
SCALE = {m: WS for m in MATS}
SCALE.update(adjT=1.0, w3=WS / 2, w4=WS / 2, w5=WS / 2, u3=WS / 2, u5=WS / 4, q2=-WS * QK, q3=-WS * QK)


def gnn_stack_kernel(nc, x, adj, adjT, w0, b0, w3T, b3, u3T, bu3, w4T, b4, w5T, b5, u5T, bu5,
                     wq, bq, wk, bk, wv, bv, wo, bo, wqkv, wproj, bproj, gamma, beta, out):
    f32, f16 = mybir.dt.float32, mybir.dt.float16
    ALU = mybir.AluOpType
    ACT = mybir.ActivationFunctionType

    x_v = x.rearrange("(g t p) d -> g p t d", t=RT, p=P)
    out_v = out.rearrange("(g t p) d -> g p t d", t=RT, p=P)

    def rows(m):
        return m.rearrange("(t p) n -> p t n", p=P)

    ctx = ExitStack()
    with ctx:
        def sb(name, shape, dt=f32):
            return ctx.enter_context(nc.sbuf_tensor(name, shape, dt))

        def sem(name):
            return ctx.enter_context(nc.semaphore(name))

        W_hi = sb("W_hi", [P, len(MATS), KT, D], f16)
        W_lo = sb("W_lo", [P, len(MATS), KT, D], f16)
        bufs = sb("bufs", [P, 10, RT, D])
        x3, tB, o_n, o_g, xbe, obe, tF, y_out, xb2, oN = (bufs[:, i] for i in range(10))
        raw = bufs[:, 0:8].rearrange("p s (m k) d -> p (s m) k d", k=KT)
        raw2 = bufs[:, 8:10].rearrange("p s (m k) d -> p (s m) k d", k=KT)
        adj_sb = sb("adj_sb", [P, KT, N])
        neg_mask = sb("neg_mask", [P, 2, KT, N])
        rep = sb("rep", [P, 5, D])
        b0_r, bo_r, bp_r, gam_r, bet_r = (rep[:, i, :] for i in range(5))
        bias_in = sb("bias_in", [P, 8, KT])
        bias = sb("bias", [P, 5, KT])
        ident = sb("ident", [P, P])
        m_half = sb("m_half", [P, RT])
        eps_t = sb("eps_t", [P, RT])
        eps4_t = sb("eps4_t", [P, RT])
        quarter = sb("quarter", [P, RT])
        xin = sb("xin", [P, RT, D])
        xb = sb("xb", [P, RT, D])
        xn_hi = sb("xn_hi", [P, RT, D], f16)
        xn_lo = sb("xn_lo", [P, RT, D], f16)
        hn_hi = sb("hn_hi", [P, RT, D], f16)
        hn_lo = sb("hn_lo", [P, RT, D], f16)
        af_hi = sb("af_hi", [P, KT, COLS], f16)
        af_lo = sb("af_lo", [P, KT, COLS], f16)
        hF = sb("hF", [P, KT, COLS])
        hf_hi = sb("hf_hi", [P, KT, COLS], f16)
        hf_lo = sb("hf_lo", [P, KT, COLS], f16)
        trb = sb("trb", [P, KT, COLS])
        tzb = sb("tzb", [P, KT, COLS])
        tvb = sb("tvb", [P, KT, COLS])
        rhb = sb("rhb", [P, KT, COLS])
        rh_hi = sb("rh_hi", [P, KT, COLS], f16)
        rh_lo = sb("rh_lo", [P, KT, COLS], f16)
        zhb = sb("zhb", [P, KT, COLS])
        keepb = sb("keepb", [P, KT, COLS])
        tA = sb("tA", [P, RT, D])
        x1 = sb("x1", [P, RT, D])
        stA = sb("stA", [P, RT, 6])
        mvA = sb("mvA", [P, RT, 2])
        veA = sb("veA", [P, RT])
        rsA = sb("rsA", [P, RT])
        x2 = sb("x2", [P, RT, D])
        xf_hi = sb("xf_hi", [P, KT, COLS], f16)
        xf_lo = sb("xf_lo", [P, KT, COLS], f16)
        q_hi = sb("q_hi", [P, KT, COLS], f16)
        q_lo = sb("q_lo", [P, KT, COLS], f16)
        k_hi = sb("k_hi", [P, KT, COLS], f16)
        k_lo = sb("k_lo", [P, KT, COLS], f16)
        qs = sb("qs", [3 * HD, H, COLS], f16)
        ks = sb("ks", [3 * HD, H, COLS], f16)
        v_hi = sb("v_hi", [P, RT, H, HD + 2], f16)
        v_lo = sb("v_lo", [P, RT, H, HD], f16)
        sp = sb("sp", [P, 3, 2, N])
        s_min = sb("s_min", [P, 3, 2])
        p_sb = sb("p_sb", [P, 3, 2, N])
        pt_hi = sb("pt_hi", [P, 3, 2 * KT * P], f16)
        pt_lo = sb("pt_lo", [P, 3, 2 * KT * P], f16)
        rec = sb("rec", [P, 2, H])
        of_hi, of_lo = q_hi, q_lo
        stB = sb("stB", [P, RT, 6])
        mvB = sb("mvB", [P, RT, 2])
        veB = sb("veB", [P, RT])
        rsB = sb("rsB", [P, RT])

        psum = [ctx.enter_context(nc.psum_tensor(f"bank{i}", [P, COLS], f32)) for i in range(8)]
        X, Y = psum[0:2], psum[2:4]
        LOW, HIGH = psum[4:6], psum[6:8]
        SC, PT, OB = psum[4], psum[5:7], psum[7]

        S = {name: sem(name) for name in PER}
        w_in_a, w_in_b, w_set, w_hi_s, w_lo_s, id_s, one_s, half_s, bias_ready, masks_ready = (
            sem(n) for n in ("w_in_a", "w_in_b", "w_set", "w_hi_done", "w_lo_done", "ident_ready", "ones_ready", "half_ready",
                             "bias_ready", "masks_ready"))
        passed = sem("passed")

        def has_before(g):
            return not isinstance(g, int) or g > 0

        def at(name, g, k):
            return g * PER[name] + k

        def settled(eng):
            eng.sem_inc(passed, 1)

        MI = {m: i for i, m in enumerate(MATS)}

        def w(m):
            i = MI[m]
            return W_hi[:, i], W_lo[:, i]

        HEAD, STEP_SLOTS = 12, 16
        A_SLOTS = HEAD + STEPS * STEP_SLOTS + 2
        LAG = 3
        AHEAD = 2
        UNIT0 = 13
        OUT0 = UNIT0 + UNITS + LAG + 1
        LAYER_SLOTS = OUT0 + 8
        B_SLOTS = 2 * LAYER_SLOTS + 5

        FOLLOW = dict(
            tensor=(3, 1, 4, 0, 0, 0, 1, 3, 0, 2, 0, 0, 0, 0, 0, 1, 1, 0, 0, 0, 1, 0, 0, 1, 1, 0, 1, 0, 1, 1,
                    0, 0, 0, 0, 0, 2, 0, 1, 4, 1, 5, 0, 0, 1, 1, 0, 0, 1, 3, 1, 0, 0, 2, 0, 0, 0, 1, 1, 0, 0,
                    0, 0, 0, 1, 0, 1, 0, 1, 0, 1, 0, 1, 0, 0, 1, 0, 0, 1, 0, 0, 0, 1, 0, 0, 1, 0, 7, 0),
            vector=(3, 1, 1, 0, 1, 2, 0, 1, 2, 1, 2, 1, 0, 0, 0, 1, 0, 0, 0, 2, 0, 0, 0, 0, 0, 0, 0, 1, 0, 0,
                    1, 0, 1, 2, 0, 0, 1, 6, 0, 1, 3, 1, 2, 0, 0, 0, 0, 3, 0, 0, 2, 0, 0, 0, 0, 3, 0, 0, 0, 0,
                    0, 1, 0, 1, 0, 0, 1, 0, 1, 0, 1, 0, 0, 1, 1, 0, 0, 0, 1, 2, 3, 0, 3, 0, 0, 1, 0, 0),
            scalar=(2, 1, 1, 0, 0, 1, 0, 0, 8, 0, 1, 1, 0, 0, 0, 0, 1, 0, 0, 0, 1, 1, 0, 0, 1, 0, 0, 0, 0, 0,
                    0, 0, 0, 2, 0, 2, 1, 1, 10, 1, 1, 0, 0, 0, 0, 0, 0, 1, 1, 2, 1, 2, 0, 0, 1, 0, 0, 0, 0, 0,
                    0, 1, 0, 0, 0, 1, 0, 1, 1, 1, 0, 0, 1, 0, 0, 0, 2, 2, 0, 0, 0, 0, 0, 1, 0, 0, 6, 0),
            gpsimd=(3, 4, 3, 1, 0, 0, 1, 0, 0, 1, 0, 0, 0, 5, 0, 0, 3, 0, 0, 0, 0, 0, 0, 3, 0, 1, 1, 0, 0, 0,
                    0, 0, 0, 1, 0, 2, 0, 1, 0, 0, 0, 1, 2, 0, 0, 0, 2, 2, 1, 0, 4, 0, 12, 0, 0, 1, 0, 0, 0, 0,
                    1, 0, 0, 0, 0, 0, 0, 0, 1, 0, 0, 0, 0, 1, 0, 0, 0, 0, 0, 0, 0, 1, 0, 2, 0, 1, 0, 0),
            sync=(0, 1, 1, 1, 0, 1, 1, 1, 0, 1, 1, 1, 0, 0, 1, 1, 0, 1, 1, 1, 0, 1, 1, 1, 0, 1, 1, 0, 1, 1,
                  1, 0, 1, 1, 1, 0, 1, 1, 0, 1, 1, 1, 0, 1, 1, 1, 0, 1, 1, 1, 0, 1, 1, 0, 0, 1, 1, 1, 0, 1,
                  1, 1, 0, 1, 1, 0, 1, 1, 1, 0, 1, 1, 1, 0, 1, 1, 0, 1, 1, 1, 0, 1, 1, 1, 0, 1, 1, 0))

        def step_of(k):
            if HEAD <= k < HEAD + STEPS * STEP_SLOTS:
                return divmod(k - HEAD, STEP_SLOTS)
            return None, None

        def layer_of(k):
            if k < 2 * LAYER_SLOTS:
                return divmod(k, LAYER_SLOTS)
            return None, None

        def unit(u):
            half, place = divmod(u, UNITS // 2)
            return place // 2, 2 * half + 4 * (place % 2), half, place % 4

        def next_group(g):
            return None if isinstance(g, int) and g == GROUPS - 1 else g + 1

        def mm3(o, l, r, start, stop, more=False):
            (lh, ll), (rh_, rl) = l, r
            nc.tensor.matmul(o, lh, rh_, start=start, stop=False, skip_group_check=more)
            nc.tensor.matmul(o, lh, rl, start=False, stop=False, skip_group_check=more)
            return nc.tensor.matmul(o, ll, rh_, start=False, stop=stop, skip_group_check=more)

        def by_feature_hi(bank, m, hi, t, k, start, stop=False, more=False):
            c = slice(t * P, t * P + P)
            nc.tensor.matmul(bank[t][:, :], w(m)[0][:, k, c], hi[:, k, :], start=start, stop=False, skip_group_check=more)
            return nc.tensor.matmul(bank[t][:, :], w(m)[1][:, k, c], hi[:, k, :], start=False, stop=stop, skip_group_check=more)

        def by_feature_lo(bank, m, lo, t, k, stop, more=False):
            return nc.tensor.matmul(bank[t][:, :], w(m)[0][:, k, t * P:t * P + P], lo[:, k, :], start=False, stop=stop,
                                    skip_group_check=more)

        def by_feature(bank, m, act, t, start, stop, more=False):
            for k in range(KT):
                by_feature_hi(bank, m, act[0], t, k, start and k == 0, False, more)
            for k in range(KT):
                last = by_feature_lo(bank, m, act[1], t, k, stop and k == KT - 1, more)
            return last

        def by_node(bank, m, act, j):
            wh, wl = w(m)
            for i in range(2):
                c = slice((2 * j + i) * P, (2 * j + i + 1) * P)
                for k in range(KT):
                    last = mm3(bank[j][:, i * D:(i + 1) * D], (act[0][:, k, c], act[1][:, k, c]),
                               (wh[:, k, :], wl[:, k, :]), k == 0, k == KT - 1)
            return last

        def adj_product(t, b, hi, lo):
            ah, al = w("adjT")
            for k in range(KT):
                r = b * KT + k
                last = mm3(X[t][:, b * N:(b + 1) * N],
                           (hi[:, r, t * P:(t + 1) * P], lo[:, r, t * P:(t + 1) * P]),
                           (ah[:, k, :], al[:, k, :]), k == 0, k == KT - 1)
            return last

        def to_features(bank, src, t):
            for r in range(RT):
                last = nc.tensor.transpose(bank[t][:, r * P:(r + 1) * P], src[:, r, t * P:(t + 1) * P], ident[:, :])
            return last

        def to_nodes(bank, src, j):
            for i in range(2):
                r = 2 * j + i
                for t in range(KT):
                    last = nc.tensor.transpose(bank[j][:, i * D + t * P:i * D + (t + 1) * P],
                                               src[:, t, r * P:(r + 1) * P], ident[:, :])
            return last

        AF = (af_hi, af_lo)

        def pe_a(pe, g, k):
            later = has_before(g)
            s, c = step_of(k)
            if k in (0, 1):
                if k == 0:
                    pe.wait_ge(S["xn_lo"], at("xn_lo", g, 2))
                    if later:
                        pe.wait_ge(S["res_a"], at("res_a", g, 0))
                for b in range(GRAPHS):
                    last = adj_product(k, b, xn_hi, xn_lo)
                last.then_inc(S["fill_x"], 1)
            if k in (4, 5):
                if k == 4:
                    pe.wait_ge(S["af_lo"], at("af_lo", g, 2))
                by_node(Y, "w0", AF, k - 4).then_inc(S["fill_y"], 1)
            if k == 9:
                pe.wait_ge(S["a_ln"], at("a_ln", g, 4))
                for t in range(KT):
                    to_features(X, x1, t).then_inc(S["fill_x"], 1)
            if s is None:
                return
            t = c % 2
            if c in (0, 1):
                pe.wait_ge(S["hn_lo"], at("hn_lo", g, 2 * s + c + 1))
                if c == 0 and s == 0:
                    pe.wait_ge(S["hf_lo"], at("hf_lo", g, 2))
                    pe.wait_ge(S["hf32"], at("hf32", g, 2))
                for f in range(KT):
                    last = adj_product(f, c, hn_hi, hn_lo)
                    if c == 1:
                        last.then_inc(S["fill_x"], 1)
            if c in (2, 3):
                for j in range(KT):
                    if c == 2:
                        pe.wait_ge(S["hf_hi"], at("hf_hi", g, 2 * s + j + 1))
                    by_feature_hi(Y, "u3", hf_hi, t, j, j == 0)
                for j in range(KT):
                    if c == 2:
                        pe.wait_ge(S["hf_lo"], at("hf_lo", g, 2 * s + j + 1))
                    by_feature_lo(Y, "u3", hf_lo, t, j, False)
            if c in (4, 5):
                for j in range(KT):
                    if c == 4:
                        pe.wait_ge(S["af_hi"], at("af_hi", g, 2 + 2 * s + j + 1))
                    by_feature_hi(Y, "w4", af_hi, t, j, False)
                for j in range(KT):
                    if c == 4:
                        pe.wait_ge(S["af_lo"], at("af_lo", g, 2 + 2 * s + j + 1))
                    last = by_feature_lo(Y, "w4", af_lo, t, j, j == KT - 1)
                last.then_inc(S["fill_y"], 1)
            if c in (6, 7):
                pe.wait_ge(S["tr"], at("tr", g, 2 * s + t + 1))
                by_feature(Y, "w3", AF, t, False, True, more=True).then_inc(S["fill_y"], 1)
            if c in (8, 9):
                by_feature(X, "w5", AF, t, True, False)
            if c in (10, 11):
                for j in range(KT):
                    if c == 10:
                        pe.wait_ge(S["rh_hi"], at("rh_hi", g, 2 * s + j + 1))
                    by_feature_hi(X, "u5", rh_hi, t, j, False)
                for j in range(KT):
                    if c == 10:
                        pe.wait_ge(S["rh_lo"], at("rh_lo", g, 2 * s + j + 1))
                    last = by_feature_lo(X, "u5", rh_lo, t, j, j == KT - 1)
                last.then_inc(S["fill_x"], 1)
            if c == 14:
                pe.wait_ge(S["hf_new"], at("hf_new", g, 2 * s + 2))
                for j in range(2):
                    to_nodes(Y, hF, j).then_inc(S["fill_y"], 1)

        def pe_b(pe, g, k):
            later = has_before(g)
            XF, OF = (xf_hi, xf_lo), (of_hi, of_lo)
            L, c = layer_of(k)
            if L is None:
                return
            wq_, wk_, wv_, wo_ = (("q2", "k2", "v2", "o2"), ("q3", "k3", "v3", "o3"))[L]
            u0 = UNITS * L
            if c == 0:
                if L == 0:
                    pe.wait_ge(S["a_ln"], at("a_ln", g, 8))
                else:
                    pe.wait_ge(S["b_ln"], at("b_ln", g, 4))
                for t in range(KT):
                    to_features(LOW, (x2, x3)[L], t).then_inc(S["xf_fill"], 1)
            if c in (3, 4):
                if c == 3:
                    if later or 2 * L > 0:
                        pe.wait_ge(S["res_b"], at("res_b", g, 2 * L))
                for j in range(KT):
                    if c == 3:
                        pe.wait_ge(S["xf_hi"], at("xf_hi", g, 2 * L + j + 1))
                    by_feature_hi(HIGH, wq_, xf_hi, c - 3, j, j == 0)
                for j in range(KT):
                    if c == 3:
                        pe.wait_ge(S["xf_lo"], at("xf_lo", g, 2 * L + j + 1))
                    last = by_feature_lo(HIGH, wq_, xf_lo, c - 3, j, j == KT - 1)
                last.then_inc(S["qk_fill"], 1)
            if c in (5, 6):
                by_feature(LOW, wk_, XF, c - 5, True, True).then_inc(S["qk_fill"], 1)
            if c in (7, 8):
                if c == 7:
                    pe.wait_ge(S["q_lo"], at("q_lo", g, 2 * L + 2))
                by_node(HIGH, wv_, XF, c - 7).then_inc(S["v_fill"], 1)
            u = c - UNIT0
            n = u + AHEAD
            if 0 <= n < UNITS:
                if n == 0:
                    pe.wait_ge(S["k_lo"], at("k_lo", g, 2 * L + 2))
                    pe.wait_ge(S["stack1"], at("stack1", g, (L + 1) * 12 * 16))
                else:
                    pe.wait_ge(S["s_min"], at("s_min", g, 2 * (u0 + n)))
                if n == UNITS // 2:
                    pe.wait_ge(S["stack2"], at("stack2", g, (L + 1) * 12 * 16))
                r, h0, half, place = unit(n)
                b = r // KT
                for j in range(2):
                    h = h0 + j
                    last = nc.tensor.matmul(SC[:, j * N:(j + 1) * N],
                                            qs[:, h, r * P:(r + 1) * P], ks[:, h, b * N:(b + 1) * N],
                                            start=True, stop=True)
                last.then_inc(S["s_fill"], 1)
            if 0 <= u - LAG < UNITS:
                w_ = u - LAG
                pe.wait_ge(S["pt_lo"], at("pt_lo", g, u0 + w_ + 1))
                r, h0, half, place = unit(w_)
                b = r // KT
                if place == 0 and w_ > 0:
                    pe.wait_ge(S["norm"], at("norm", g, RT * L + w_ // 4))
                for j in range(2):
                    h = h0 + j
                    o_ = OB[:, (2 * place + j) * (HD + 1):(2 * place + j + 1) * (HD + 1)]
                    for m in range(KT):
                        i = j * KT + m
                        ph = pt_hi[:, w_ % 3, i * P:(i + 1) * P]
                        pl = pt_lo[:, w_ % 3, i * P:(i + 1) * P]
                        vr = b * KT + m
                        nc.tensor.matmul(o_, ph, v_hi[:, vr, h, 0:HD + 1], start=m == 0, stop=False)
                        nc.tensor.matmul(o_[:, 0:HD], ph, v_lo[:, vr, h, :], start=False, stop=False)
                        last = nc.tensor.matmul(o_, pl, v_hi[:, vr, h, 0:HD + 1], start=False, stop=m == KT - 1)
                last.then_inc(S["pv"], 1)
            if 0 <= u < UNITS:
                pe.wait_ge(S["p_exp"], at("p_exp", g, 2 * (u0 + u + 1)))
                if u == 0:
                    pe.wait_ge(S["v_lo"], at("v_lo", g, 2 * L + 2))
                elif u > 1:
                    if later or u0 + u - 1 > 0:
                        pe.wait_ge(S["pt_lo"], at("pt_lo", g, u0 + u - 1))
                for j in range(2):
                    for m in range(KT):
                        i = j * KT + m
                        last = nc.tensor.transpose(PT[u % 2][:, i * P:(i + 1) * P],
                                                   p_sb[:, u % 3, j, m * P:(m + 1) * P], ident[:, :])
                last.then_inc(S["pt_fill"], 1)
            if c == OUT0:
                pe.wait_ge(S["norm"], at("norm", g, RT * (L + 1)))
                for t in range(KT):
                    to_features(LOW, oN, t).then_inc(S["of_fill"], 1)
            if c in (OUT0 + 3, OUT0 + 4):
                if c == OUT0 + 3:
                    pe.wait_ge(S["of_lo"], at("of_lo", g, 2 * L + 2))
                by_node(HIGH, wo_, OF, c - OUT0 - 3).then_inc(S["o_fill"], 1)

        def split_x_hi(act, g):
            later = has_before(g)
            if g is None:
                return
            act.wait_ge(S["x_loaded"], at("x_loaded", g, 16))
            if later or 2 - PER["fill_x"] > 0:
                act.wait_ge(S["fill_x"], at("fill_x", g, 2 - PER["fill_x"]))
            for j in range(2):
                nc.scalar.activation(xn_hi[:, 2 * j:2 * j + 2, :], xin[:, 2 * j:2 * j + 2, :], ACT.Copy).then_inc(S["xn_hi"], 1)

        def act_a(act, g, k):
            later = has_before(g)
            A = nc.scalar.activation
            s, c = step_of(k)
            if k in (1, 2):
                act.wait_ge(S["fill_x"], at("fill_x", g, k))
                A(af_hi[:, k - 1, :], X[k - 1][:, :], ACT.Copy).then_inc(S["af_hi"], 1)
            if k == 9:
                act.wait_ge(S["a_ln"], at("a_ln", g, 4))
                for j in range(2):
                    A(hn_hi[:, 2 * j:2 * j + 2, :], x1[:, 2 * j:2 * j + 2, :], ACT.Copy).then_inc(S["hn_hi"], 1)
            if k == 10:
                for t in range(KT):
                    act.wait_ge(S["fill_x"], at("fill_x", g, 2 + t + 1))
                    A(hf_hi[:, t, :], X[t][:, :], ACT.Copy).then_inc(S["hf_hi"], 1)
                    A(hF[:, t, :], X[t][:, :], ACT.Copy).then_inc(S["hf32"], 1)
            if s is None:
                return
            fx = 4 + 4 * s
            fy = 2 + 6 * s
            if c in (1, 2):
                t = c - 1
                act.wait_ge(S["fill_x"], at("fill_x", g, fx + t + 1))
                A(af_hi[:, t, :], X[t][:, :], ACT.Copy).then_inc(S["af_hi"], 1)
            if s == 1 and c == 4:
                split_x_hi(act, next_group(g))
            if c in (5, 6):
                t = c - 5
                act.wait_ge(S["fill_y"], at("fill_y", g, fy + t + 1))
                A(trb[:, t, :], Y[t][:, :], ACT.Tanh, bias=bias[:, 1, t:t + 1], scale=0.5 / WS).then_inc(S["tr"], 1)
            if c in (7, 8):
                t = c - 7
                act.wait_ge(S["rh"], at("rh", g, 2 * s + t + 1))
                A(rh_hi[:, t, :], rhb[:, t, :], ACT.Copy).then_inc(S["rh_hi"], 1)
                act.wait_ge(S["fill_y"], at("fill_y", g, fy + 2 + t + 1))
                A(tzb[:, t, :], Y[t][:, :], ACT.Tanh, bias=bias[:, 0, t:t + 1], scale=0.5 / WS).then_inc(S["tz"], 1)
            if c in (11, 12):
                t = c - 11
                act.wait_ge(S["fill_x"], at("fill_x", g, fx + 2 + t + 1))
                A(tvb[:, t, :], X[t][:, :], ACT.Tanh, bias=bias[:, 2, t:t + 1], scale=1.0 / WS).then_inc(S["tv"], 1)
            if c in (13, 14) and s < STEPS - 1:
                t = c - 13
                act.wait_ge(S["hf_new"], at("hf_new", g, 2 * s + t + 1))
                A(hf_hi[:, t, :], hF[:, t, :], ACT.Copy).then_inc(S["hf_hi"], 1)
            if c == 15 and s < STEPS - 1:
                for j in range(2):
                    act.wait_ge(S["fill_y"], at("fill_y", g, fy + 4 + j + 1))
                    A(hn_hi[:, 2 * j:2 * j + 2, :], Y[j][:, :].rearrange("p (a b) -> p a b", a=2), ACT.Copy).then_inc(S["hn_hi"], 1)

        def act_b(act, g, k):
            later = has_before(g)
            A = nc.scalar.activation
            L, c = layer_of(k)
            if L is None:
                return
            u0 = UNITS * L
            if c == 1:
                for t in range(KT):
                    act.wait_ge(S["xf_fill"], at("xf_fill", g, 2 * L + t + 1))
                    A(xf_hi[:, t, :], LOW[t][:, :], ACT.Copy).then_inc(S["xf_hi"], 1)
            if c in (4, 5, 6, 7):
                m, t = divmod(c - 4, 2)
                name, buf, bank = (("q_hi", q_hi, HIGH), ("k_hi", k_hi, LOW))[m]
                act.wait_ge(S["qk_fill"], at("qk_fill", g, 4 * L + 2 * m + t + 1))
                if L == 0:
                    A(buf[:, t, :], bank[t][:, :], ACT.Identity, bias=bias[:, 3 + m, t:t + 1], scale=1.0).then_inc(S[name], 1)
                else:
                    A(buf[:, t, :], bank[t][:, :], ACT.Copy).then_inc(S[name], 1)
            if c in (8, 9):
                j = c - 8
                act.wait_ge(S["v_fill"], at("v_fill", g, 2 * L + j + 1))
                A(v_hi[:, 2 * j:2 * j + 2, :, 0:HD].rearrange("p a h d -> p (a h) d"),
                  HIGH[j][:, :].rearrange("p (h d) -> p h d", d=HD), ACT.Copy, scale=1.0 / WS).then_inc(S["v_hi"], 1)
            u = c - UNIT0
            if 0 <= u - 1 < UNITS:
                if later or u0 + u - 3 > 0:
                    act.wait_ge(S["pv"], at("pv", g, u0 + u - 3))
                act.wait_ge(S["pt_fill"], at("pt_fill", g, u0 + u))
                A(pt_hi[:, (u - 1) % 3, :], PT[(u - 1) % 2][:, :], ACT.Copy).then_inc(S["pt_hi"], 1)
            n = u + AHEAD
            if 0 <= n < UNITS:
                if later or u0 + n - 2 > 0:
                    act.wait_ge(S["pt_fill"], at("pt_fill", g, u0 + n - 2))
                for j in range(2):
                    act.wait_ge(S["s_min"], at("s_min", g, 2 * (u0 + n) + j + 1))
                    A(p_sb[:, n % 3, j, :], sp[:, n % 3, j, :], ACT.Exp, bias=s_min[:, n % 3, j:j + 1], scale=-1.0).then_inc(S["p_exp"], 1)
            if c == OUT0 + 1:
                for t in range(KT):
                    act.wait_ge(S["of_fill"], at("of_fill", g, 2 * L + t + 1))
                    if L == 0:
                        A(of_hi[:, t, :], LOW[t][:, :], ACT.Identity, bias=bias_in[:, 7, t:t + 1], scale=1.0).then_inc(S["of_hi"], 1)
                    else:
                        A(of_hi[:, t, :], LOW[t][:, :], ACT.Copy).then_inc(S["of_hi"], 1)

        V = nc.vector

        def stats(dve, src, st, mv, names, g, n):
            later = has_before(g)
            s_st, s_mv, s_ve = names
            if later or RT * n > 0:
                dve.wait_ge(S[s_mv], at(s_mv, g, RT * n))
            for r in range(RT):
                V.bn_stats(st[:, r, :], src[:, r, :]).then_inc(S[s_st], 1)
            dve.wait_ge(S[s_st], at(s_st, g, RT * (n + 1)))
            settled(dve)
            for r in range(RT):
                V.bn_aggr(mv[:, r, :], st[:, r, :]).then_inc(S[s_mv], 1)

        def normalise(dve, dst, src, mv, rs, names, g, n):
            later = has_before(g)
            s_rs, s_ln = names
            dve.wait_ge(S[s_rs], at(s_rs, g, n + 1))
            for r in range(RT):
                V.tensor_scalar(dst[:, r, :], src[:, r, :], mv[:, r, 0:1], rs[:, r:r + 1],
                                ALU.subtract, ALU.mult).then_inc(S[s_ln], 1)

        def low_part(dve, name, lo, src, hi):
            V.tensor_tensor(lo, src, hi, ALU.subtract).then_inc(S[name], 1)

        def dve_a(dve, g, k):
            later = has_before(g)
            s, c = step_of(k)
            if k in (2, 3):
                dve.wait_ge(S["af_hi"], at("af_hi", g, k - 1))
                low_part(dve, "af_lo", af_lo[:, k - 2, :], X[k - 2][:, :], af_hi[:, k - 2, :])
            if k in (5, 6):
                j = k - 5
                dve.wait_ge(S["xb"], at("xb", g, 1))
                dve.wait_ge(S["fill_y"], at("fill_y", g, j + 1))
                V.scalar_tensor_tensor(out=tA[:, 2 * j:2 * j + 2, :].rearrange("p a b -> p (a b)"), in0=Y[j][:, :], scalar=1.0 / WS,
                                       in1=xb[:, 2 * j:2 * j + 2, :].rearrange("p a b -> p (a b)"),
                                       op0=ALU.mult, op1=ALU.add).then_inc(S["res_a"], 1)
                if j == 1:
                    dve.wait_ge(S["res_a"], at("res_a", g, 2))
                    stats(dve, tA, stA, mvA, ("a_st", "a_mv", "a_ve"), g, 0)
            if k == 8:
                normalise(dve, x1, tA, mvA, rsA, ("a_rs", "a_ln"), g, 0)
            if k == 11:
                for t in range(KT):
                    dve.wait_ge(S["hf32"], at("hf32", g, t + 1))
                    low_part(dve, "hf_lo", hf_lo[:, t, :], X[t][:, :], hf_hi[:, t, :])
            if k == A_SLOTS - 1:
                if later:
                    dve.wait_ge(S["xb2"], at("xb2", g, 0))
                if later:
                    dve.wait_ge(S["xf_fill"], at("xf_fill", g, -2))
                normalise(dve, x2, tA, mvA, rsA, ("a_rs", "a_ln"), g, 1)
            if s is None:
                return
            fy = 2 + 6 * s
            t = c % 2
            if c in (2, 3):
                dve.wait_ge(S["af_hi"], at("af_hi", g, 2 + 2 * s + t + 1))
                low_part(dve, "af_lo", af_lo[:, t, :], X[t][:, :], af_hi[:, t, :])
            if c in (6, 7):
                dve.wait_ge(S["tr"], at("tr", g, 2 * s + t + 1))
                V.scalar_tensor_tensor(out=rhb[:, t, :], in0=trb[:, t, :], scalar=1.0, in1=hF[:, t, :],
                                       op0=ALU.add, op1=ALU.mult).then_inc(S["rh"], 1)
            if c in (8, 9):
                dve.wait_ge(S["rh_hi"], at("rh_hi", g, 2 * s + t + 1))
                low_part(dve, "rh_lo", rh_lo[:, t, :], rhb[:, t, :], rh_hi[:, t, :])
            if c in (12, 13):
                dve.wait_ge(S["tz"], at("tz", g, 2 * s + t + 1))
                dve.wait_ge(S["tv"], at("tv", g, 2 * s + t + 1))
                V.scalar_tensor_tensor(out=tvb[:, t, :], in0=tzb[:, t, :], scalar=1.0, in1=tvb[:, t, :],
                                       op0=ALU.add, op1=ALU.mult).then_inc(S["zv"], 1)
                dve.wait_ge(S["keep"], at("keep", g, 2 * s + t + 1))
                dve.wait_ge(S["zv"], at("zv", g, 2 * s + t + 1))
                V.scalar_tensor_tensor(out=hF[:, t, :], in0=keepb[:, t, :], scalar=0.5, in1=tvb[:, t, :],
                                       op0=ALU.mult, op1=ALU.add).then_inc(S["hf_new"], 1)
            if c == 15 and s < STEPS - 1:
                for j in range(2):
                    dve.wait_ge(S["hn_hi"], at("hn_hi", g, 2 + 2 * s + j + 1))
                    low_part(dve, "hn_lo", hn_lo[:, 2 * j:2 * j + 2, :].rearrange("p a b -> p (a b)"), Y[j][:, :],
                             hn_hi[:, 2 * j:2 * j + 2, :].rearrange("p a b -> p (a b)"))
            if c == 15 and s == STEPS - 1:
                for j in range(2):
                    dve.wait_ge(S["fill_y"], at("fill_y", g, fy + 4 + j + 1))
                    V.tensor_tensor(tA[:, 2 * j:2 * j + 2, :].rearrange("p a b -> p (a b)"), Y[j][:, :],
                                    x1[:, 2 * j:2 * j + 2, :].rearrange("p a b -> p (a b)"), ALU.add).then_inc(S["res_a"], 1)
                dve.wait_ge(S["res_a"], at("res_a", g, 4))
                stats(dve, tA, stA, mvA, ("a_st", "a_mv", "a_ve"), g, 1)

        def dve_b(dve, g, k):
            later = has_before(g)
            L, c = layer_of(k)
            names = ("b_st", "b_mv", "b_ve")
            if k == 2 * LAYER_SLOTS + 1:
                dve.wait_ge(S["gam"], at("gam", g, 1))
                V.tensor_tensor(tF[:, :, :], o_g[:, :, :], obe[:, :, :], ALU.add).then_inc(S["t_fin"], 1)
                dve.wait_ge(S["t_fin"], at("t_fin", g, 1))
                stats(dve, tF, stB, mvB, names, g, 2)
            if k == 2 * LAYER_SLOTS + 3:
                if later:
                    dve.wait_ge(S["stored"], at("stored", g, 0))
                normalise(dve, y_out, tF, mvB, rsB, ("b_rs", "b_ln"), g, 2)
            if L is None:
                return
            u0 = UNITS * L
            if c == 2:
                for t in range(KT):
                    dve.wait_ge(S["xf_hi"], at("xf_hi", g, 2 * L + t + 1))
                    low_part(dve, "xf_lo", xf_lo[:, t, :], LOW[t][:, :], xf_hi[:, t, :])
            if c in (5, 6, 7, 8):
                m, t = divmod(c - 5, 2)
                his, los, hi, lo, bank = (("q_hi", "q_lo", q_hi, q_lo, HIGH), ("k_hi", "k_lo", k_hi, k_lo, LOW))[m]
                dve.wait_ge(S[his], at(his, g, 2 * L + t + 1))
                if L == 0:
                    V.scalar_tensor_tensor(out=lo[:, t, :], in0=bank[t][:, :], scalar=bias[:, 3 + m, t:t + 1],
                                           in1=hi[:, t, :], op0=ALU.add, op1=ALU.subtract).then_inc(S[los], 1)
                else:
                    low_part(dve, los, lo[:, t, :], bank[t][:, :], hi[:, t, :])
            if c in (9, 10):
                j = c - 9
                dve.wait_ge(S["v_hi"], at("v_hi", g, 2 * L + j + 1))
                V.scalar_tensor_tensor(out=v_lo[:, 2 * j:2 * j + 2, :, :].rearrange("p a h d -> p (a h) d"),
                                       in0=HIGH[j][:, :].rearrange("p (h d) -> p h d", d=HD), scalar=1.0 / WS,
                                       in1=v_hi[:, 2 * j:2 * j + 2, :, 0:HD].rearrange("p a h d -> p (a h) d"),
                                       op0=ALU.mult, op1=ALU.subtract).then_inc(S["v_lo"], 1)
            u = c - UNIT0
            n = u + AHEAD
            if 0 <= n < UNITS:
                if later or 2 * (u0 + n) - 4 > 0:
                    dve.wait_ge(S["p_exp"], at("p_exp", g, 2 * (u0 + n) - 4))
                dve.wait_ge(S["s_fill"], at("s_fill", g, u0 + n + 1))
                settled(dve)
                for j in range(2):
                    V.tensor_tensor_reduce(out=sp[:, n % 3, j, :], in0=SC[:, j * N:(j + 1) * N],
                                           in1=neg_mask[:, L, unit(n)[0] % KT, :], scale=1.0 / (WS * WS), scalar=3.0e38,
                                           op0=ALU.add, op1=ALU.min,
                                           accum_out=s_min[:, n % 3, j:j + 1]).then_inc(S["s_min"], 1)
            if 0 <= u - 1 < UNITS:
                dve.wait_ge(S["pt_hi"], at("pt_hi", g, u0 + u))
                low_part(dve, "pt_lo", pt_lo[:, (u - 1) % 3, :], PT[(u - 1) % 2][:, :], pt_hi[:, (u - 1) % 3, :])
            if u >= LAG and (u - LAG) % 4 == 3 and u - LAG < UNITS:
                n = (u - LAG) // 4
                r, h0, half, place = unit(u - LAG)
                o_ = OB[:, 0:H * (HD + 1)].rearrange("p (h d) -> p h d", d=HD + 1)
                dve.wait_ge(S["pv"], at("pv", g, u0 + u - LAG + 1))
                V.reciprocal(rec[:, n % 2, :], o_[:, :, HD]).then_inc(S["rec"], 1)
                dve.wait_ge(S["rec"], at("rec", g, RT * L + n + 1))
                V.tensor_tensor(oN[:, r - 1:r + 1, :].rearrange("p r (a f j d) -> p (r a) f j d", a=2, f=2, j=2)[:, :, half],
                                OB[:, 0:H * (HD + 1)].rearrange("p (w j d) -> p w j d", w=4, j=2)[:, :, :, 0:HD],
                                rec[:, n % 2, :].rearrange("p (w j) -> p w j", j=2).unsqueeze(3).to_broadcast([P, 4, 2, HD]),
                                ALU.mult).then_inc(S["norm"], 1)
            if c == OUT0 + 2:
                for t in range(KT):
                    dve.wait_ge(S["of_hi"], at("of_hi", g, 2 * L + t + 1))
                    if L == 0:
                        V.scalar_tensor_tensor(out=of_lo[:, t, :], in0=LOW[t][:, :], scalar=bias_in[:, 7, t:t + 1],
                                               in1=of_hi[:, t, :], op0=ALU.add, op1=ALU.subtract).then_inc(S["of_lo"], 1)
                    else:
                        low_part(dve, "of_lo", of_lo[:, t, :], LOW[t][:, :], of_hi[:, t, :])
            if c in (OUT0 + 4, OUT0 + 5):
                j = c - OUT0 - 4
                if L == 0:
                    dve.wait_ge(S["xb2"], at("xb2", g, 1))
                    if later:
                        dve.wait_ge(S["obe"], at("obe", g, 0))
                dve.wait_ge(S["o_fill"], at("o_fill", g, 2 * L + j + 1))
                if L == 0:
                    V.scalar_tensor_tensor(out=tB[:, 2 * j:2 * j + 2, :].rearrange("p a b -> p (a b)"), in0=HIGH[j][:, :],
                                           scalar=1.0 / WS, in1=xb2[:, 2 * j:2 * j + 2, :].rearrange("p a b -> p (a b)"),
                                           op0=ALU.mult, op1=ALU.add).then_inc(S["res_b"], 1)
                else:
                    V.scalar_tensor_tensor(out=tB[:, 2 * j:2 * j + 2, :], in0=HIGH[j][:, :].rearrange("p (a b) -> p a b", a=2),
                                           scalar=1.0 / WS, in1=bp_r.unsqueeze(1).to_broadcast([P, 2, D]),
                                           op0=ALU.mult, op1=ALU.add).then_inc(S["res_b"], 1)
                if j == 1:
                    dve.wait_ge(S["res_b"], at("res_b", g, 2 * L + 2))
                    stats(dve, tB, stB, mvB, names, g, L)
            if c == LAYER_SLOTS - 1:
                if L == 0:
                    normalise(dve, x3, tB, mvB, rsB, ("b_rs", "b_ln"), g, 0)
                else:
                    normalise(dve, o_n, tB, mvB, rsB, ("b_rs", "b_ln"), g, 1)

        G = nc.gpsimd

        def rstd(pool, mv, ve, rs, names, g, n):
            later = has_before(g)
            s_mv, s_ve, s_rs = names
            pool.wait_ge(S[s_mv], at(s_mv, g, RT * (n + 1)))
            if later or n > 0:
                pool.wait_ge(S[s_rs], at(s_rs, g, n))
            G.tensor_tensor(ve[:, :], mv[:, :, 1], eps_t[:, :], ALU.add).then_inc(S[s_ve], 1)
            pool.wait_ge(S[s_ve], at(s_ve, g, n + 1))
            G.tensor_tensor(rs[:, :], ve[:, :], m_half[:, :], ALU.pow).then_inc(S[s_rs], 1)

        def add_bias(pool, g):
            later = has_before(g)
            if g is None:
                return
            pool.wait_ge(S["x_loaded"], at("x_loaded", g, 16))
            if later:
                pool.wait_ge(S["res_a"], at("res_a", g, -2))
            G.tensor_tensor(xb[:, :, :], xin[:, :, :], b0_r.unsqueeze(1).to_broadcast([P, RT, D]), ALU.add).then_inc(S["xb"], 1)

        def split_x_lo(pool, g):
            later = has_before(g)
            if g is None:
                return
            for j in range(2):
                pool.wait_ge(S["xn_hi"], at("xn_hi", g, j + 1))
                G.tensor_tensor(xn_lo[:, 2 * j:2 * j + 2, :], xin[:, 2 * j:2 * j + 2, :], xn_hi[:, 2 * j:2 * j + 2, :],
                                ALU.subtract).then_inc(S["xn_lo"], 1)

        def pool_a(pool, g, k):
            later = has_before(g)
            s, c = step_of(k)
            if k == 7:
                pool.wait_ge(S["a_mv"], at("a_mv", g, RT))
                if later:
                    pool.wait_ge(S["a_rs"], at("a_rs", g, 0))
                G.tensor_tensor(veA[:, :], mvA[:, :, 1], eps_t[:, :], ALU.add).then_inc(S["a_ve"], 1)
                pool.wait_ge(S["a_ve"], at("a_ve", g, 1))
                G.tensor_tensor(veA[:, :], veA[:, :], quarter[:, :], ALU.mult).then_inc(S["a_ve"], 1)
                pool.wait_ge(S["a_ve"], at("a_ve", g, 2))
                G.tensor_tensor(rsA[:, :], veA[:, :], m_half[:, :], ALU.pow).then_inc(S["a_rs"], 1)
            if k == 10:
                for j in range(2):
                    pool.wait_ge(S["hn_hi"], at("hn_hi", g, j + 1))
                    G.tensor_tensor(hn_lo[:, 2 * j:2 * j + 2, :], x1[:, 2 * j:2 * j + 2, :], hn_hi[:, 2 * j:2 * j + 2, :],
                                    ALU.subtract).then_inc(S["hn_lo"], 1)
            if k == A_SLOTS - 2:
                pool.wait_ge(S["a_mv"], at("a_mv", g, 2 * RT))
                pool.wait_ge(S["a_rs"], at("a_rs", g, 1))
                G.tensor_tensor(veA[:, :], mvA[:, :, 1], eps4_t[:, :], ALU.add).then_inc(S["a_ve"], 1)
                pool.wait_ge(S["a_ve"], at("a_ve", g, 3))
                G.tensor_tensor(rsA[:, :], veA[:, :], m_half[:, :], ALU.pow).then_inc(S["a_rs"], 1)
            if s is None:
                return
            if s == 1 and c == 5:
                split_x_lo(pool, next_group(g))
                add_bias(pool, next_group(g))
            if c in (9, 10):
                t = c - 9
                pool.wait_ge(S["tz"], at("tz", g, 2 * s + t + 1))
                G.tensor_tensor(zhb[:, t, :], tzb[:, t, :], hF[:, t, :], ALU.mult).then_inc(S["zh"], 1)
                pool.wait_ge(S["zh"], at("zh", g, 2 * s + t + 1))
                G.tensor_tensor(keepb[:, t, :], hF[:, t, :], zhb[:, t, :], ALU.subtract).then_inc(S["keep"], 1)
            if c in (14, 15) and s < STEPS - 1:
                t = c - 14
                pool.wait_ge(S["hf_hi"], at("hf_hi", g, 2 + 2 * s + t + 1))
                G.tensor_tensor(hf_lo[:, t, :], hF[:, t, :], hf_hi[:, t, :], ALU.subtract).then_inc(S["hf_lo"], 1)

        def pool_b(pool, g, k):
            later = has_before(g)
            names = ("b_mv", "b_ve", "b_rs")
            if k == 0:
                pool.wait_ge(S["a_ln"], at("a_ln", g, 8))
                G.tensor_tensor(xb2[:, :, :], x2[:, :, :], bo_r.unsqueeze(1).to_broadcast([P, RT, D]), ALU.add).then_inc(S["xb2"], 1)
            if k == LAYER_SLOTS - 2:
                rstd(pool, mvB, veB, rsB, names, g, 0)
            if k == LAYER_SLOTS + 1:
                pool.wait_ge(S["b_ln"], at("b_ln", g, 4))
                G.tensor_tensor(xbe[:, :, :], x3[:, :, :], bet_r.unsqueeze(1).to_broadcast([P, RT, D]), ALU.add).then_inc(S["xbe"], 1)
            if k == 2 * LAYER_SLOTS - 2:
                rstd(pool, mvB, veB, rsB, names, g, 1)
                pool.wait_ge(S["res_b"], at("res_b", g, 4))
                pool.wait_ge(S["xbe"], at("xbe", g, 1))
                G.tensor_tensor(obe[:, :, :], xbe[:, :, :], tB[:, :, :], ALU.add).then_inc(S["obe"], 1)
            if k == 2 * LAYER_SLOTS:
                pool.wait_ge(S["b_ln"], at("b_ln", g, 8))
                G.tensor_tensor(o_g[:, :, :], o_n[:, :, :], gam_r.unsqueeze(1).to_broadcast([P, RT, D]), ALU.mult).then_inc(S["gam"], 1)
            if k == 2 * LAYER_SLOTS + 2:
                rstd(pool, mvB, veB, rsB, names, g, 2)

        def load_x(sp_, g):
            later = has_before(g)
            if later:
                sp_.wait_ge(S["xn_hi"], at("xn_hi", g, 0))
            if later:
                sp_.wait_ge(S["xn_lo"], at("xn_lo", g, 0))
            if later:
                sp_.wait_ge(S["xb"], at("xb", g, 0))
            settled(sp_)
            sp_.dma_start(xin[:, :, :], x_v[g]).then_inc(S["x_loaded"], 16)

        def sp_a(sp_, g, k):
            later = has_before(g)
            if k == 8 and next_group(g) is not None:
                load_x(sp_, next_group(g))

        def sp_b(sp_, g, k):
            later = has_before(g)
            L, c = layer_of(k)
            if k == 2 * LAYER_SLOTS + 4:
                sp_.wait_ge(S["b_ln"], at("b_ln", g, 12))
                settled(sp_)
                sp_.dma_start(out_v[g], y_out[:, :, :]).then_inc(S["stored"], 16)
            if L is not None and c in (7, 9):
                Q = (qs, (q_hi, q_hi, q_lo))
                K = (ks, (k_hi, k_lo, k_hi))
                low = "q_lo" if c == 7 else "k_lo"
                sp_.wait_ge(S[low], at(low, g, 2 * L + 2))
                for (dst, parts), half in (((Q, 0),) if c == 7 else ((K, 0), (Q, 1), (K, 1))):
                    for i in (2 * half, 2 * half + 1):
                        for m, src in enumerate(parts):
                            sp_.dma_start(dst[m * HD:(m + 1) * HD, i:H:P // HD, :],
                                          src[i * HD:(i + 1) * HD, :, :]).then_inc(S[("stack1", "stack2")[half]], 16)

        def merged(eng, follow, a, ga, b, gb):
            done = 0
            for i, more in enumerate(follow):
                if i > 0:
                    b(eng, gb, i - 1)
                for k in range(done, done + more):
                    a(eng, ga, k)
                done += more

        def whole(eng, follow, a, b, prepare):
            for k in range(A_SLOTS):
                a(eng, 0, k)
                prepare(eng, k)
            merged(eng, follow, a, 1, b, 0)
            with eng.Fori(2, GROUPS - 1) as g:
                merged(eng, follow, a, g, b, g - 1)
            merged(eng, follow, a, GROUPS - 1, b, GROUPS - 2)
            for k in range(B_SLOTS):
                b(eng, GROUPS - 1, k)

        MATS_A = MATS.index("q2")
        PREP0 = HEAD + STEP_SLOTS // 2

        def prepared(k):
            i, rest = divmod(k - PREP0, 3)
            return MATS_A + i if k >= PREP0 and rest == 0 and MATS_A + i < len(MATS) else None

        def split_hi(act, i):
            nc.scalar.activation(W_hi[:, i], raw[:, i], ACT.Copy, scale=SCALE[MATS[i]]).then_inc(w_hi_s, 1)

        def split_lo(dve, i):
            dve.wait_ge(w_hi_s, i + 1)
            V.scalar_tensor_tensor(out=W_lo[:, i], in0=raw[:, i], scalar=SCALE[MATS[i]], in1=W_hi[:, i],
                                   op0=ALU.mult, op1=ALU.subtract).then_inc(w_lo_s, 1)

        def prepare_sp(sp_, k):
            pass

        def prepare_pe(pe, k):
            if k == A_SLOTS - 1:
                pe.wait_ge(w_lo_s, len(MATS))
                pe.wait_ge(one_s, 1)

        def prepare_act(act, k):
            if k == PREP0 - 1:
                act.wait_ge(w_in_b, IN_B * 16)
            if prepared(k) is not None:
                split_hi(act, prepared(k))
            if k == A_SLOTS - 1:
                act.wait_ge(masks_ready, 5)

        def prepare_dve(dve, k):
            if k == PREP0 - 1:
                dve.wait_ge(w_in_b, IN_B * 16)
            if prepared(k) is not None:
                split_lo(dve, prepared(k))
            if k == A_SLOTS - 4:
                V.tensor_scalar(neg_mask[:, 0], adj_sb[:, :, :], -1.0, 1.0, ALU.mult, ALU.add).then_inc(masks_ready, 1)
                V.tensor_scalar(neg_mask[:, 1], adj_sb[:, :, :], 0.0, MASK_L3, ALU.is_equal, ALU.mult).then_inc(masks_ready, 1)
                V.tensor_scalar(bias[:, 3, :], bias_in[:, 5, :], -WS * QK, None, ALU.mult).then_inc(masks_ready, 1)
                V.tensor_scalar(bias[:, 4, :], bias_in[:, 6, :], WS, None, ALU.mult).then_inc(masks_ready, 1)
                dve.wait_ge(masks_ready, 4)
                V.tensor_scalar(neg_mask[:, 0], neg_mask[:, 0], MASK_L2 * WS * WS, None, ALU.mult).then_inc(masks_ready, 1)
            if k == A_SLOTS - 1:
                dve.wait_ge(masks_ready, 5)
                dve.wait_ge(one_s, 1)

        def prepare_pool(pool, k):
            if k == A_SLOTS - 1:
                pool.wait_ge(w_in_b, IN_B * 16)

        block = ctx.enter_context(nc.Block())

        @block.sync
        def _(sp_):
            load_x(sp_, 0)
            plain = [adjT, w0, w3T[0:D, :], w4T[0:D, :], w5T[0:D, :], u3T, u5T, wq, wk, wv, wo,
                     wqkv[:, 0:D], wqkv[:, D:2 * D], wqkv[:, 2 * D:3 * D], wproj]
            reps = (b0, bo, bproj, gamma, beta)
            small = (b3, b4, b5, bu3, bu5, bq, bk, bv)
            for i in range(MATS_A):
                sp_.dma_start(raw[:, i], rows(plain[i])).then_inc(w_in_a, 16)
            for i, m in enumerate((w3T, w4T, w5T)):
                sp_.dma_start(raw2[:, i], rows(m[D:2 * D, :])).then_inc(w_in_a, 16)
            sp_.dma_start(rep[:, 0, :], reps[0].rearrange("(a n) -> a n", a=1).to_broadcast([P, D])).then_inc(w_in_a, 16)
            for i in range(5):
                sp_.dma_start(bias_in[:, i, :], small[i].rearrange("(t p) -> p t", p=P), allow_slow_non_contiguous=True).then_inc(w_in_a, 16)
            for i in range(MATS_A, len(MATS)):
                sp_.dma_start(raw[:, i], rows(plain[i])).then_inc(w_in_b, 16)
            sp_.dma_start(adj_sb[:, :, :], rows(adj)).then_inc(w_in_b, 16)
            for i in range(1, 5):
                sp_.dma_start(rep[:, i, :], reps[i].rearrange("(a n) -> a n", a=1).to_broadcast([P, D])).then_inc(w_in_b, 16)
            for i in range(5, 8):
                sp_.dma_start(bias_in[:, i, :], small[i].rearrange("(t p) -> p t", p=P), allow_slow_non_contiguous=True).then_inc(w_in_b, 16)
            whole(sp_, FOLLOW["sync"], sp_a, sp_b, prepare_sp)
            sp_.wait_ge(S["stored"], GROUPS * 16)

        IN_A = MATS_A + 3 + 1 + 5
        IN_B = len(MATS) - MATS_A + 1 + 4 + 3

        @block.tensor
        def _(pe):
            pe.wait_ge(id_s, 2)
            pe.wait_ge(w_lo_s, MATS_A)
            whole(pe, FOLLOW["tensor"], pe_a, pe_b, prepare_pe)

        @block.scalar
        def _(act):
            act.wait_ge(w_in_a, IN_A * 16)
            for i in range(MATS_A):
                if MATS[i] in ("w3", "w4", "w5"):
                    act.wait_ge(w_set, 4)
                split_hi(act, i)
            act.wait_ge(bias_ready, 4)
            split_x_hi(act, 0)
            whole(act, FOLLOW["scalar"], act_a, act_b, prepare_act)

        @block.vector
        def _(dve):
            V.memset(v_hi[:, :, :, :], 1.0).then_inc(one_s, 1)
            dve.wait_ge(w_in_a, IN_A * 16)
            for i in range(3):
                V.tensor_tensor(raw[:, 2 + i], raw[:, 2 + i], raw2[:, i], ALU.add).then_inc(w_set, 1)
            dve.wait_ge(w_set, 3)
            V.tensor_tensor(raw[:, 2], raw[:, 2], raw[:, 3], ALU.subtract).then_inc(w_set, 1)
            dve.wait_ge(w_set, 4)
            V.tensor_tensor(bias[:, 0, :], bias_in[:, 0, :], bias_in[:, 3, :], ALU.add).then_inc(bias_ready, 1)
            V.tensor_tensor(bias[:, 1, :], bias_in[:, 1, :], bias_in[:, 3, :], ALU.add).then_inc(bias_ready, 1)
            V.tensor_tensor(bias[:, 2, :], bias_in[:, 2, :], bias_in[:, 4, :], ALU.add).then_inc(bias_ready, 1)
            dve.wait_ge(bias_ready, 3)
            V.tensor_scalar(bias[:, 0:2, :], bias[:, 0:2, :], 0.5, None, ALU.mult).then_inc(bias_ready, 1)
            for i in range(MATS_A):
                split_lo(dve, i)
            whole(dve, FOLLOW["vector"], dve_a, dve_b, prepare_dve)

        @block.gpsimd
        def _(pool):
            G.memset(ident[:, :], 0.0).then_inc(id_s, 1)
            G.memset(m_half[:, :], -0.5).then_inc(half_s, 1)
            G.memset(eps_t[:, :], EPS).then_inc(half_s, 1)
            G.memset(eps4_t[:, :], 4 * EPS).then_inc(half_s, 1)
            G.memset(quarter[:, :], 0.25).then_inc(half_s, 1)
            pool.wait_ge(id_s, 1)
            G.affine_select(out=ident[:, :], in_=ident[:, :], compare_op=ALU.not_equal, fill=1.0, base=0,
                            pattern=[[-1, P]], channel_multiplier=1).then_inc(id_s, 1)
            pool.wait_ge(half_s, 4)
            pool.wait_ge(w_in_a, IN_A * 16)
            split_x_lo(pool, 0)
            add_bias(pool, 0)
            whole(pool, FOLLOW["gpsimd"], pool_a, pool_b, prepare_pool)


def kernel(**inputs):
    import numpy as np
    import concourse.bacc as bacc
    from concourse import mybir as _mybir
    from concourse.bass_utils import run_bass_kernel_spmd

    def a(name):
        return np.ascontiguousarray(inputs[name])

    def t(name):
        return np.ascontiguousarray(np.asarray(inputs[name]).T)

    arrays = dict(
        x=a("x").reshape(B * N, D), adj=a("adj"), adjT=t("adj"), w0=a("L0_gnn_weight"), b0=a("L0_gnn_bias"),
        w3T=t("L1_gnn_w3_w"), b3=a("L1_gnn_w3_b"), u3T=t("L1_gnn_u3_w"), bu3=a("L1_gnn_u3_b"),
        w4T=t("L1_gnn_w4_w"), b4=a("L1_gnn_w4_b"), w5T=t("L1_gnn_w5_w"), b5=a("L1_gnn_w5_b"),
        u5T=t("L1_gnn_u5_w"), bu5=a("L1_gnn_u5_b"),
        wq=a("L2_gnn_Wq"), bq=a("L2_gnn_bq"), wk=a("L2_gnn_Wk"), bk=a("L2_gnn_bk"),
        wv=a("L2_gnn_Wv"), bv=a("L2_gnn_bv"), wo=a("L2_gnn_Wo"), bo=a("L2_gnn_bo"),
        wqkv=a("L3_gnn_w_qkv"), wproj=a("L3_gnn_w_proj"), bproj=a("L3_gnn_b_proj"),
        gamma=a("L3_gnn_ln_gamma"), beta=a("L3_gnn_ln_beta"))
    nc = bacc.Bacc("TRN2", target_bir_lowering=False, num_devices=1)
    args = [nc.dram_tensor(f"in_{n}", v.shape, _mybir.dt.from_np(v.dtype), kind="ExternalInput").ap() for n, v in arrays.items()]
    args.append(nc.dram_tensor("out", (B * N, D), _mybir.dt.float32, kind="ExternalOutput").ap())
    gnn_stack_kernel(nc, *args)
    r = run_bass_kernel_spmd(nc, [{f"in_{n}": v for n, v in arrays.items()}], core_ids=[0])
    return r.results[0]["out"].reshape(B, N, D)
```
